# Optimizing a Trainium2 kernel written in Bass

```python
import numpy as np
import jax
import jax.numpy as jnp

def _softmax(x, axis=-1):
    return jax.nn.softmax(x, axis=axis)

def _gelu(x):
    return jax.nn.gelu(x, approximate=True)

def _silu(x):
    return jax.nn.silu(x)

def _sigmoid(x):
    return jax.nn.sigmoid(x)

def _layernorm(x, axis=-1, eps=1e-05):
    m = jnp.mean(x, axis=axis, keepdims=True)
    v = jnp.var(x, axis=axis, keepdims=True)
    return (x - m) / jnp.sqrt(v + eps)

def _scatter_add(tgt, idx, src, axis=0):
    return tgt.at[idx].add(src)

def _segment_sum(src, seg, n):
    return jax.ops.segment_sum(src, seg, n)
kernel_name = 'mk_gnn_preln_d1_gnn_r32_52af74'

def setup_inputs(seed: int=0):
    np.random.seed(seed)
    _w = jnp.asarray

    def _rec_inputs():
        import jax
        import jax.numpy as jnp
        _gk = jax.random.key(seed)
        x = 7.22e-05 + 1 * jax.random.normal(jax.random.fold_in(_gk, 1), (512, 512), jnp.float32)
        src = jax.random.randint(jax.random.fold_in(_gk, 2), (8192,), 0, 512, jnp.int32)
        dst = jnp.minimum((512 * jax.random.uniform(jax.random.fold_in(_gk, 3), (8192,)) ** 2.0).astype(jnp.int32), 16383)
        _o = jnp.argsort(dst, stable=True)
        src = src[_o]
        dst = dst[_o]
        return (x, src, dst)
    x, src, dst = _rec_inputs()

    def _L0_gnn_setup():
        import jax, jax.numpy as jnp
        import numpy as np
        N, D, BS, M, DC, H, DH, L, E = (512, 512, 16, 256, 512, 8, 64, 4, 8192)
        EPS = 1e-05

        def _ln(x, w, b):
            mu = jnp.mean(x, -1, keepdims=True)
            var = jnp.var(x, -1, keepdims=True)
            return (x - mu) * jax.lax.rsqrt(var + EPS) * w + b

        def _gcn(x, src, dst, W, b, n):
            deg = jax.ops.segment_sum(jnp.ones_like(src, dtype=x.dtype), dst, num_segments=n)
            dinv = jnp.where(deg > 0, deg ** (-0.5), 0.0)
            norm = dinv[src] * dinv[dst]
            h = x @ W
            out = jax.ops.segment_sum(h[src] * norm[:, None], dst, num_segments=n)
            return out + b

        def _attn(xf, cond, Wq, Wk, Wv, Wo):
            n, d = xf.shape
            xb = xf.reshape(BS, n // BS, d)
            q = (xb @ Wq).reshape(BS, -1, H, DH)
            k = (cond @ Wk).reshape(BS, -1, H, DH)
            v = (cond @ Wv).reshape(BS, -1, H, DH)
            att = jnp.einsum('bnhd,bmhd->bhnm', q, k) * DH ** (-0.5)
            w = jax.nn.softmax(att, axis=-1)
            o = jnp.einsum('bhnm,bmhd->bnhd', w, v).reshape(BS, -1, H * DH)
            return (o @ Wo).reshape(n, d)
        key = jax.random.key(seed)
        ks = jax.random.split(key, 24)
        s = lambda fi, fo: (2.0 / (fi + fo)) ** 0.5
        inp = {'x': jax.random.normal(ks[0], (N, D), jnp.float32), 'edge_index': jax.random.randint(ks[1], (2, E), 0, N, jnp.int64), 'cond': jax.random.normal(ks[2], (BS, M, DC), jnp.float32), 'bn_w': jnp.ones((D,), jnp.float32), 'bn_b': jnp.zeros((D,), jnp.float32), 'gcn_in_w': jax.random.normal(ks[3], (D, D), jnp.float32) * s(D, D), 'gcn_in_b': jnp.zeros((D,), jnp.float32), 'gcn_out_w': jax.random.normal(ks[4], (D, D), jnp.float32) * s(D, D), 'gcn_out_b': jnp.zeros((D,), jnp.float32), 'Wq': jax.random.normal(ks[5], (L, D, H * DH), jnp.float32) * s(D, H * DH), 'Wk': jax.random.normal(ks[6], (L, DC, H * DH), jnp.float32) * s(DC, H * DH), 'Wv': jax.random.normal(ks[7], (L, DC, H * DH), jnp.float32) * s(DC, H * DH), 'Wo': jax.random.normal(ks[8], (L, H * DH, D), jnp.float32) * s(H * DH, D), 'ln2_w': jnp.ones((L, D), jnp.float32), 'ln2_b': jnp.zeros((L, D), jnp.float32), 'ln3_w': jnp.ones((L, D), jnp.float32), 'ln3_b': jnp.zeros((L, D), jnp.float32), 'geglu_w': jax.random.normal(ks[9], (L, D, 8 * D), jnp.float32) * s(D, 8 * D), 'geglu_b': jnp.zeros((L, 8 * D), jnp.float32), 'ffo_w': jax.random.normal(ks[10], (L, 4 * D, D), jnp.float32) * s(4 * D, D), 'ffo_b': jnp.zeros((L, D), jnp.float32)}
        return inp
    _L0_gnn_all = _L0_gnn_setup()
    _L0_gnn_in = {k: v for k, v in _L0_gnn_all.items() if k in ('cond', 'bn_w', 'bn_b', 'gcn_in_w', 'gcn_in_b', 'gcn_out_w', 'gcn_out_b', 'Wq', 'Wk', 'Wv', 'Wo', 'ln2_w', 'ln2_b', 'ln3_w', 'ln3_b', 'geglu_w', 'geglu_b', 'ffo_w', 'ffo_b')}
    del _L0_gnn_all
    return {'x': x, 'src': src, 'dst': dst, 'L0_gnn_cond': _L0_gnn_in['cond'], 'L0_gnn_bn_w': _L0_gnn_in['bn_w'], 'L0_gnn_bn_b': _L0_gnn_in['bn_b'], 'L0_gnn_gcn_in_w': _L0_gnn_in['gcn_in_w'], 'L0_gnn_gcn_in_b': _L0_gnn_in['gcn_in_b'], 'L0_gnn_gcn_out_w': _L0_gnn_in['gcn_out_w'], 'L0_gnn_gcn_out_b': _L0_gnn_in['gcn_out_b'], 'L0_gnn_Wq': _L0_gnn_in['Wq'], 'L0_gnn_Wk': _L0_gnn_in['Wk'], 'L0_gnn_Wv': _L0_gnn_in['Wv'], 'L0_gnn_Wo': _L0_gnn_in['Wo'], 'L0_gnn_ln2_w': _L0_gnn_in['ln2_w'], 'L0_gnn_ln2_b': _L0_gnn_in['ln2_b'], 'L0_gnn_ln3_w': _L0_gnn_in['ln3_w'], 'L0_gnn_ln3_b': _L0_gnn_in['ln3_b'], 'L0_gnn_geglu_w': _L0_gnn_in['geglu_w'], 'L0_gnn_geglu_b': _L0_gnn_in['geglu_b'], 'L0_gnn_ffo_w': _L0_gnn_in['ffo_w'], 'L0_gnn_ffo_b': _L0_gnn_in['ffo_b']}

def reference(x, src, dst, L0_gnn_cond, L0_gnn_bn_w, L0_gnn_bn_b, L0_gnn_gcn_in_w, L0_gnn_gcn_in_b, L0_gnn_gcn_out_w, L0_gnn_gcn_out_b, L0_gnn_Wq, L0_gnn_Wk, L0_gnn_Wv, L0_gnn_Wo, L0_gnn_ln2_w, L0_gnn_ln2_b, L0_gnn_ln3_w, L0_gnn_ln3_b, L0_gnn_geglu_w, L0_gnn_geglu_b, L0_gnn_ffo_w, L0_gnn_ffo_b):
    import jax
    import jax.numpy as jnp

    def _L0_gnn_ref(x, edge_index, cond, bn_w, bn_b, gcn_in_w, gcn_in_b, gcn_out_w, gcn_out_b, Wq, Wk, Wv, Wo, ln2_w, ln2_b, ln3_w, ln3_b, geglu_w, geglu_b, ffo_w, ffo_b):
        import jax, jax.numpy as jnp
        import numpy as np
        N, D, BS, M, DC, H, DH, L, E = (512, 512, 16, 256, 512, 8, 64, 4, 8192)
        EPS = 1e-05

        def _ln(x, w, b):
            mu = jnp.mean(x, -1, keepdims=True)
            var = jnp.var(x, -1, keepdims=True)
            return (x - mu) * jax.lax.rsqrt(var + EPS) * w + b

        def _gcn(x, src, dst, W, b, n):
            deg = jax.ops.segment_sum(jnp.ones_like(src, dtype=x.dtype), dst, num_segments=n)
            dinv = jnp.where(deg > 0, deg ** (-0.5), 0.0)
            norm = dinv[src] * dinv[dst]
            h = x @ W
            out = jax.ops.segment_sum(h[src] * norm[:, None], dst, num_segments=n)
            return out + b

        def _attn(xf, cond, Wq, Wk, Wv, Wo):
            n, d = xf.shape
            xb = xf.reshape(BS, n // BS, d)
            q = (xb @ Wq).reshape(BS, -1, H, DH)
            k = (cond @ Wk).reshape(BS, -1, H, DH)
            v = (cond @ Wv).reshape(BS, -1, H, DH)
            att = jnp.einsum('bnhd,bmhd->bhnm', q, k) * DH ** (-0.5)
            w = jax.nn.softmax(att, axis=-1)
            o = jnp.einsum('bhnm,bmhd->bnhd', w, v).reshape(BS, -1, H * DH)
            return (o @ Wo).reshape(n, d)
        n = x.shape[0]
        loops = jnp.arange(n)
        src = jnp.concatenate([edge_index[0], loops])
        dst = jnp.concatenate([edge_index[1], loops])
        x_in = x
        mu = jnp.mean(x, 0)
        var = jnp.var(x, 0)
        h = (x - mu) * jax.lax.rsqrt(var + EPS) * bn_w + bn_b
        h = _gcn(h, src, dst, gcn_in_w, gcn_in_b, n)
        for i in range(L):
            a = _attn(_ln(h, ln2_w[i], ln2_b[i]), cond, Wq[i], Wk[i], Wv[i], Wo[i])
            h = h + a
            u = _ln(h, ln3_w[i], ln3_b[i]) @ geglu_w[i] + geglu_b[i]
            val, gate = jnp.split(u, 2, axis=-1)
            f = val * jax.nn.gelu(gate, approximate=False)
            h = h + f @ ffo_w[i] + ffo_b[i]
        h = _gcn(h, src, dst, gcn_out_w, gcn_out_b, n)
        return h + x_in
    edge_index = jnp.stack([src, dst])
    h = jnp.maximum(_layernorm(x, axis=-1), 0.0)
    x = x + _L0_gnn_ref(h, edge_index, L0_gnn_cond, L0_gnn_bn_w, L0_gnn_bn_b, L0_gnn_gcn_in_w, L0_gnn_gcn_in_b, L0_gnn_gcn_out_w, L0_gnn_gcn_out_b, L0_gnn_Wq, L0_gnn_Wk, L0_gnn_Wv, L0_gnn_Wo, L0_gnn_ln2_w, L0_gnn_ln2_b, L0_gnn_ln3_w, L0_gnn_ln3_b, L0_gnn_geglu_w, L0_gnn_geglu_b, L0_gnn_ffo_w, L0_gnn_ffo_b)
    return x

_drawn_inputs = setup_inputs


def setup_inputs(seed=0):
    import zlib

    import numpy as np

    out = dict(_drawn_inputs(seed))
    spreads = {'L0_gnn_bn_w': (1.0, 0.6),
     'L0_gnn_bn_b': (0.0, 0.1),
     'L0_gnn_gcn_in_b': (0.0, 0.1),
     'L0_gnn_gcn_out_b': (0.0, 0.1),
     'L0_gnn_ln2_w': (1.0, 0.6),
     'L0_gnn_ln2_b': (0.0, 0.8),
     'L0_gnn_ln3_w': (1.0, 0.539),
     'L0_gnn_ln3_b': (0.0, 0.38),
     'L0_gnn_geglu_b': (0.0, 0.1),
     'L0_gnn_ffo_b': (0.0, 0.1)}
    factors = {}
    for name, (base, spread) in spreads.items():
        noise = np.random.default_rng([zlib.crc32(name.encode()), seed]).standard_normal(out[name].shape)
        drawn = base * np.exp(spread * noise) if base else spread * noise
        out[name] = jnp.asarray(drawn.astype(out[name].dtype))
    for name, factor in factors.items():
        out[name] = (out[name] * factor).astype(out[name].dtype)
    return out
```

```python
import concourse.bass as bass
from concourse import mybir
from contextlib import ExitStack

P = 128
N, D = 512, 512
BS, M = 16, 256
H, DH = 8, 64
L, E = 4, 8192
F = 4 * D
EPS = 1e-5
NB = N // BS
NC = N // P
DC = D // P
HALVES = 2
HN = N // HALVES
HB = BS // HALVES
HP = H // 2
TILE = 2048
HT = TILE // 2
FI = 4
FJ = F // P // FI
LT = 4 + 3 * FI
NT = 2 + L * LT
EC = E // P
EG = 4
UNITS = DC * HP


def build(nc, x, src, dst, tiles, cond_n, cond_t, bn_p, ln_p, gb_p, rows, out, adj_hi, adj_lo, rest):
    f32, f32r = mybir.dt.float32, mybir.dt.float32r
    bf16, f16, i32 = mybir.dt.bfloat16, mybir.dt.float16, mybir.dt.int32
    ALU, ACT, AX = mybir.AluOpType, mybir.ActivationFunctionType, mybir.AxisListType

    ctx = ExitStack()
    with ctx:
        def sb(name, shape, dt):
            return ctx.enter_context(nc.sbuf_tensor(name, shape, dt))

        def sem(name):
            return ctx.enter_context(nc.semaphore(name))

        slot_hi = [sb(f"slot_hi{s}", [P, TILE], f32r) for s in range(3)]
        slot_lo = [sb(f"slot_lo{s}", [P, TILE], f32r) for s in range(3)]
        SA, SB_, SC = 0, 1, 2
        w_raw = sb("w_raw", [P, 2, HT], f32)
        qz_hi = sb("qz_hi", [P, DC * H * HN], f32r)
        qz_lo = sb("qz_lo", [P, DC * H * HN], f32r)
        qz = [t[:, :].rearrange("p (d b h n) -> p d b h n", d=DC, b=HB, h=H) for t in (qz_hi, qz_lo)]
        def part(t, n):
            return t[:, n * TILE:(n + 1) * TILE].rearrange("p (c n) -> p c n", n=512)
        y_hi, y_lo = part(qz_hi, 0), part(qz_lo, 0)
        fT_hi, fT_lo = part(qz_hi, 1), part(qz_lo, 1)
        adjh, adjl = part(qz_hi, 1), part(qz_lo, 1)
        u_hi, u_lo = part(qz_hi, 2), part(qz_lo, 2)
        ct_raw = sb("ct_raw", [P, DC, M], f32)
        cn_raw = sb("cn_raw", [P, 2, D], f32)
        ct_in_at = [ct_raw[:, :, :], w_raw[:, 0, :].rearrange("p (c m) -> p c m", c=DC)]
        cn_in_at = [cn_raw[:, :, :], w_raw[:, 1, :].rearrange("p (c n) -> p c n", c=2)]
        ct_hi = sb("ct_hi", [P, 2, DC, M], f32r)
        ct_lo = sb("ct_lo", [P, 2, DC, M], f32r)
        cn_hi = sb("cn_hi", [P, 2, 2, D], f32r)
        cn_lo = sb("cn_lo", [P, 2, 2, D], f32r)
        q_f = sb("q_f", [P, HP, N], f32)
        onehot = q_f[:, :, :].bitcast(bf16).rearrange("p a (b n) -> p (a b) n", n=512)
        gelu = q_f[:, 0:2, :]
        prod = q_f[:, 2:4, :]
        q_hi = sb("q_hi", [P, HP, HN], f32r)
        q_lo = sb("q_lo", [P, HP, HN], f32r)
        o_hi, o_lo = (t[:, 0, :, :].rearrange("p c n -> p (c n)").rearrange("p (j n) -> p j n", j=HP) for t in (cn_hi, cn_lo))
        h = sb("h", [P, NC, D], f32)
        xn = sb("xn", [P, NC, D], f32)
        ex = sb("ex", [P, 2, 2, M], f32)
        y_f = ex[:, :, :, :].rearrange("p a b m -> p a (b m)")
        w_hi = sb("w_hi", [P, 2, 2 * P], f32r)
        w_lo = sb("w_lo", [P, 2, 2 * P], f32r)
        bias_row = sb("bias_row", [P, D], f32)
        iota = bias_row[:, 0:D // 2].bitcast(f16)
        ident = sb("ident", [P, P], f32)
        identb = sb("identb", [P, P], bf16)
        zrow = sb("zrow", [1, D], bf16)
        ones_f = sb("ones_f", [P, 2], f32)
        ones = sb("ones", [P, 2], f32r)
        edge_i = sb("edge_i", [P, 2, EC], i32)
        edge_f = sb("edge_f", [P, 2, EC], f32)
        bn_s = sb("bn_s", [P, DC, 2], f32)
        ln_s = sb("ln_s", [P, L * 2 * DC * 2], f32)
        gb_s = sb("gb_s", [P, L * FI * FJ * 2], f32)
        stats = sb("stats", [P, 4, 6], f32)
        mv = sb("mv", [P, 4, 2], f32)
        vare = sb("vare", [P, 4], f32)
        mhalf = sb("mhalf", [P, 4], f32)
        epsc = sb("epsc", [P, 4], f32)
        rstd = sb("rstd", [P, 4], f32)
        deg = sb("deg", [P, NC], f32)
        degp = sb("degp", [P, NC], f32)
        has = sb("has", [P, NC], f32)
        dinv = sb("dinv", [P, NC], f32)
        nmax = sb("nmax", [P, 2, 2], f32)
        esum = sb("esum", [P, 2, 2], f32)
        rsum = sb("rsum", [P, 2, 2], f32)

        ps = ctx.enter_context(nc.psum_tensor("ps", [P, 8, 512], f32))
        psf = ps[:, :, :].rearrange("p b n -> p (b n)")

        x_in, e_in, p_in, row_in = sem("x_in"), sem("e_in"), sem("p_in"), sem("row_in")
        raw_in = [sem("raw_in0"), sem("raw_in1")]
        ct_in, cn_in = [sem("ct_in0"), sem("ct_in1")], [sem("cn_in0"), sem("cn_in1")]
        adj_out, rest_out, back_in, out_done = sem("adj_out"), sem("rest_out"), sem("back_in"), sem("out_done")
        whi_made, wlo_made = sem("whi_made"), sem("wlo_made")
        cthi_made, ctlo_made, cnhi_made, cnlo_made = (sem(n) for n in ("cthi_made", "ctlo_made", "cnhi_made", "cnlo_made"))
        const_made, onehot_made, onehot_free, adj_done = (sem(n) for n in ("const_made", "onehot_made", "onehot_free", "adj_done"))
        adjhi_made, adjlo_made, deg_done, dinv_step, pow_made = (sem(n) for n in ("adjhi_made", "adjlo_made", "deg_done", "dinv_step", "pow_made"))
        u_done, uhi_made, ulo_made, g_done = (sem(n) for n in ("u_done", "uhi_made", "ulo_made", "g_done"))
        passed = sem("passed")
        pre = sem("pre")
        bns = sem("bns")
        h_new, stat_made, mv_made, rstd_step, rstd_made, xn_made = (sem(n) for n in ("h_new", "stat_made", "mv_made", "rstd_step", "rstd_made", "xn_made"))
        turned, yf_made, yhi_made, ylo_made = (sem(n) for n in ("turned", "yf_made", "yhi_made", "ylo_made"))
        q_done, qf_made, qhi_made, qlo_made = (sem(n) for n in ("q_done", "qf_made", "qhi_made", "qlo_made"))
        qk_done, qkhi_made, qklo_made = (sem(n) for n in ("qk_done", "qkhi_made", "qklo_made"))
        s_done, max_made, exp_made, rsum_made, p_made = (sem(n) for n in ("s_done", "max_made", "exp_made", "rsum_made", "p_made"))
        t_done, phi_made, plo_made = (sem(n) for n in ("t_done", "phi_made", "plo_made"))
        z_done, zhi_made, zlo_made = (sem(n) for n in ("z_done", "zhi_made", "zlo_made"))
        o_done, ohi_made, olo_made, wo_done = (sem(n) for n in ("o_done", "ohi_made", "olo_made", "wo_done"))
        gate_done, val_done, gelu_made, prod_made, fhi_made, flo_made, ff_done, bias_added = (
            sem(n) for n in ("gate_done", "val_done", "gelu_made", "prod_made", "fhi_made", "flo_made", "ff_done", "bias_added"))

        block = ctx.enter_context(nc.Block())

        def alone(eng):
            eng.sem_inc(passed, 1)

        def tile_of(l, k):
            return l * LT + (1 + k)

        def z_at(w, b):
            return qz[w][:, :, b, :, :].rearrange("p d h n -> p d (h n)")

        def unit_at(w, u):
            dc, first = u % 8 // 2, 4 * (u // 8) + u % 2
            return qz[w][:, dc, :, first:first + 3:2, :].rearrange("p b e n -> p e b n")

        def bank_of(u):
            return ps[:, u % 8, :].rearrange("p (e b n) -> p e b n", e=2, b=HB)

        def split3(hi_a, lo_a, hi_b, lo_b):
            return ((hi_a, hi_b), (lo_a, hi_b), (hi_a, lo_b))

        @block.sync
        def _(sp):
            def load_tile(t):
                for k in range(2):
                    if not (isinstance(t, int) and t == 0):
                        sp.wait_ge(wlo_made, t * 2 + (k - 1))
                    sp.dma_start(w_raw[:, k, :], tiles[t, :, k * HT:(k + 1) * HT]).then_inc(raw_in[k], 16)

            sp.dma_start(h[:, :, :], x.rearrange("(c p) n -> p c n", p=P)).then_inc(x_in, 16)
            sp.dma_start(edge_i[:, 0, :], src.rearrange("(p c) -> p c", p=P)).then_inc(e_in, 16)
            sp.dma_start(edge_i[:, 1, :], dst.rearrange("(p c) -> p c", p=P)).then_inc(e_in, 16)
            sp.dma_start(bn_s[:, :, :], bn_p).then_inc(p_in, 16)
            sp.dma_start(ln_s[:, :], ln_p).then_inc(p_in, 16)
            sp.dma_start(gb_s[:, :], gb_p).then_inc(p_in, 16)
            sp.dma_start(y_f[:, 1, :], rows[L + 1:L + 2, :].broadcast_to([P, D])).then_inc(row_in, 16)
            load_tile(0)
            load_tile(1)
            sp.wait_ge(pre, 3 * NC + 1)
            sp.dma_start(rest[:, 0:2, :], cn_raw[:, :, :]).then_inc(rest_out, 16)
            sp.dma_start(rest[:, 2:4, :], ct_raw[:, :, :].rearrange("p a b -> p (a b)").rearrange("p (a b) -> p a b", b=D)).then_inc(rest_out, 16)
            sp.wait_ge(onehot_made, 2 * EC)
            sp.dma_start(bias_row[:, :], rows[0:1, :].broadcast_to([P, D])).then_inc(row_in, 16)
            sp.wait_ge(adjlo_made, NC)
            sp.dma_start(adj_hi, adjh.bitcast(f32)).then_inc(adj_out, 16)
            sp.dma_start(adj_lo, adjl.bitcast(f32)).then_inc(adj_out, 16)
            sp.wait_ge(rest_out, 32)
            sp.wait_ge(adj_out, 32)
            sp.wait_ge(h_new, NC)

            with sp.Fori(0, L) as l:
                for k in (1, 2, 3):
                    load_tile(tile_of(l, k))
                with sp.Fori(0, HALVES) as hf:
                    nb = l * BS + hf * HB

                    def load_ct(b):
                        if b == 1:
                            sp.wait_ge(wlo_made, (tile_of(l, 3) + 1) * 2)
                        if b >= 2:
                            sp.wait_ge(ctlo_made, nb + (b - 1))
                        sp.dma_start(ct_in_at[b % 2], cond_t[hf, b, :, :].rearrange("p (c m) -> p c m", c=DC)).then_inc(ct_in[b % 2], 16)

                    def load_cn(b):
                        if b >= 2:
                            sp.wait_ge(cnlo_made, nb + (b - 1))
                        sp.dma_start(cn_in_at[b % 2], cond_n[hf, b, :, :].rearrange("p (c n) -> p c n", c=2)).then_inc(cn_in[b % 2], 16)

                    load_ct(0)
                    load_cn(0)
                    load_ct(1)
                    load_cn(1)
                    load_ct(2)
                    for b in range(HB):
                        if b + 3 < HB:
                            load_ct(b + 3)
                        if b + 2 < HB:
                            load_cn(b + 2)
                    sp.wait_ge(ctlo_made, nb + HB)
                    alone(sp)
                    sp.wait_ge(cnlo_made, nb + HB)
                    alone(sp)
                load_tile(tile_of(l, 4))
                sp.dma_start(bias_row[:, :], rows[l + 1, :].unsqueeze(0).broadcast_to([P, D])).then_inc(row_in, 16)
                with sp.Fori(0, FI) as i:
                    for k in (5, 6, 7):
                        load_tile(tile_of(l, k) + i * 3)

            sp.wait_ge(ff_done, L * FI * NC)
            sp.dma_start(adjh.bitcast(f32), adj_hi).then_inc(back_in, 16)
            sp.dma_start(adjl.bitcast(f32), adj_lo).then_inc(back_in, 16)
            sp.wait_ge(xn_made, 8 * L + 2 * NC)
            sp.dma_start(xn[:, :, :], rest).then_inc(back_in, 16)
            for c in range(NC):
                sp.wait_ge(h_new, 4 + 8 * L + c + 1)
                sp.dma_start(out.rearrange("(c p) n -> p c n", p=P)[:, c, :], h[:, c, :]).then_inc(out_done, 16)
            sp.wait_ge(out_done, 16 * NC)

        @block.gpsimd
        def _(pool):
            nc.gpsimd.iota(iota, [[1, D]], base=0, channel_multiplier=0,
                           allow_small_or_imprecise_dtypes=True).then_inc(const_made, 1)
            nc.gpsimd.memset(zrow[:, :], 0.0).then_inc(const_made, 1)
            nc.gpsimd.memset(ones_f[:, :], 1.0).then_inc(const_made, 1)
            nc.gpsimd.memset(mhalf[:, :], -0.5).then_inc(const_made, 1)
            nc.gpsimd.memset(epsc[:, :], EPS).then_inc(const_made, 1)
            nc.gpsimd.memset(ident[:, :], 0.0).then_inc(const_made, 1)
            pool.wait_ge(const_made, 6)
            nc.gpsimd.affine_select(out=ident[:, :], in_=ident[:, :], compare_op=ALU.not_equal, fill=1.0,
                                    base=0, pattern=[[-1, P]], channel_multiplier=1).then_inc(const_made, 1)

            def power(ln, k, steps=1):
                pool.wait_ge(mv_made, ln + 1)
                nc.gpsimd.tensor_tensor(vare[:, k:k + steps], mv[:, k:k + steps, 1], epsc[:, k:k + steps], ALU.add).then_inc(rstd_step, 1)
                pool.wait_ge(rstd_step, ln + 1)
                nc.gpsimd.tensor_tensor(rstd[:, k:k + steps], vare[:, k:k + steps], mhalf[:, k:k + steps], ALU.pow).then_inc(rstd_made, 1)

            for c in range(NC):
                power(c, c)
            power(NC, 0, DC)
            pool.wait_ge(dinv_step, 2)
            nc.gpsimd.tensor_tensor(dinv[:, :], degp[:, :], mhalf[:, :], ALU.pow).then_inc(pow_made, 1)
            for c in range(NC):
                power(NC + 1 + c, c)
            with pool.Fori(0, L) as l:
                ln0 = l * 8 + (2 * NC + 1)
                with pool.Fori(0, HALVES) as hf:
                    nb = l * BS + hf * HB
                    for b in range(HB):
                        pool.wait_ge(rsum_made, nb + (b + 1))
                        nc.gpsimd.tensor_tensor(ex[:, b % 2, :, :], ex[:, b % 2, :, :],
                                                rsum[:, b % 2, :].unsqueeze(2).broadcast_to([P, 2, M]), ALU.mult).then_inc(p_made, 1)
                    for c in range(2):
                        power(ln0 + hf * 2 + c, c)
                pool.wait_ge(row_in, 16 * 3 + l * 16)
                pool.wait_ge(xn_made, l * 8 + 12)
                for c in range(NC):
                    nc.gpsimd.tensor_tensor(h[:, c, :], h[:, c, :], bias_row[:, :], ALU.add).then_inc(bias_added, 1)
                for c in range(NC):
                    power(ln0 + (4 + c), c)

        @block.scalar
        def _(act):
            def split_hi(t, slot, used=None, value=0):
                for k in range(2):
                    act.wait_ge(raw_in[k], t * 16 + 16)
                    if k == 0 and used is not None:
                        act.wait_ge(used, value)
                    nc.scalar.activation(slot_hi[slot][:, k * HT:(k + 1) * HT], w_raw[:, k, :], ACT.Copy).then_inc(whi_made, 1)

            def y_high(first):
                for dc in range(DC):
                    act.wait_ge(yf_made, first + (dc + 1))
                    nc.scalar.activation(y_hi[:, dc, :], y_f[:, dc % 2, :], ACT.Copy).then_inc(yhi_made, 1)

            def u_high(first, bank):
                for c in range(NC):
                    act.wait_ge(u_done, first + c + 1)
                    nc.scalar.activation(u_hi[:, c, :], ps[:, bank + c, :], ACT.Copy, scale=dinv[:, c:c + 1]).then_inc(uhi_made, 1)

            act.wait_ge(const_made, 7)
            nc.scalar.activation(identb[:, :], ident[:, :], ACT.Copy).then_inc(const_made, 1)
            nc.scalar.activation(ones[:, :], ones_f[:, :], ACT.Copy).then_inc(const_made, 1)
            split_hi(0, SC)
            y_high(0)
            split_hi(1, SB_)
            for c in range(NC):
                act.wait_ge(adj_done, c + 1)
                nc.scalar.activation(adjh[:, c, :], ps[:, 4 + c, :], ACT.Copy).then_inc(adjhi_made, 1)
            act.wait_ge(dinv_step, 4)
            u_high(0, 0)

            with act.Fori(0, L) as l:
                y_high(l * 8 + 4)
                split_hi(tile_of(l, 1), SC)
                split_hi(tile_of(l, 2), SA)

                def q_high(g, start, count):
                    act.wait_ge(qf_made, count)
                    nc.scalar.activation(q_hi[:, 2 * g:2 * g + 2, :], q_f[:, 2 * g:2 * g + 2, bass.ds(start, HN)], ACT.Copy).then_inc(qhi_made, 1)

                for j in range(HP):
                    act.wait_ge(q_done, l * HP + (j + 1))
                    nc.scalar.activation(q_f[:, j, :], ps[:, 4 + j, :], ACT.Copy, scale=DH ** -0.5).then_inc(qf_made, 1)
                    if j % 2:
                        q_high(j // 2, 0, l * HP + (j + 1))
                split_hi(tile_of(l, 3), SB_, q_done, l * HP + HP)
                with act.Fori(0, HALVES) as hf:
                    hh = l * 2 + hf
                    nb = hh * HB

                    def ct_high(b):
                        act.wait_ge(ct_in[b % 2], (hh * (HB // 2) + (b // 2 + 1)) * 16)
                        if b >= 2:
                            act.wait_ge(s_done, nb + (b - 1))
                        nc.scalar.activation(ct_hi[:, b % 2, :, :], ct_in_at[b % 2], ACT.Copy).then_inc(cthi_made, 1)

                    def cn_high(b):
                        act.wait_ge(cn_in[b % 2], (hh * (HB // 2) + (b // 2 + 1)) * 16)
                        if b >= 2:
                            act.wait_ge(z_done, nb + (b - 1))
                        nc.scalar.activation(cn_hi[:, b % 2, :, :], cn_in_at[b % 2], ACT.Copy).then_inc(cnhi_made, 1)

                    def exps(b):
                        act.wait_ge(max_made, nb + (b + 1))
                        for k in range(2):
                            nc.scalar.activation(ex[:, b % 2, k, :], ps[:, b % 2, k * M:(k + 1) * M], ACT.Exp,
                                                 bias=nmax[:, b % 2, k:k + 1], accum_out=esum[:, b % 2, k:k + 1]).then_inc(exp_made, 1)

                    def p_high(b):
                        act.wait_ge(t_done, nb + (b + 1))
                        nc.scalar.activation(w_hi[:, :, :], ps[:, 2, :].rearrange("p (a b) -> p a b", a=2), ACT.Copy).then_inc(phi_made, 1)

                    def z_high(b):
                        act.wait_ge(z_done, nb + (b + 1))
                        bank = 4 + 2 * (b % 2)
                        nc.scalar.activation(z_at(0, b), psf[:, bank * 512:(bank + 2) * 512].rearrange("p (d n) -> p d n", n=H * NB),
                                             ACT.Copy).then_inc(zhi_made, 1)

                    for u in range(UNITS):
                        act.wait_ge(qk_done, hh * UNITS + (u + 1))
                        nc.scalar.activation(unit_at(0, u), bank_of(u), ACT.Copy).then_inc(qkhi_made, 1)
                        if u == 1:
                            ct_high(0)
                        if u == 5:
                            ct_high(1)
                        if u == 9:
                            cn_high(0)
                    exps(0)
                    ct_high(2)
                    exps(1)
                    for b in range(HB):
                        p_high(b)
                        if b >= 1:
                            z_high(b - 1)
                        if b + 3 < HB:
                            ct_high(b + 3)
                        if b + 1 < HB:
                            cn_high(b + 1)
                        if b + 2 < HB:
                            exps(b + 2)
                        if b == HB - 2:
                            for g in range(2):
                                q_high(g, HN - hf * HN, l * HP + HP)
                    z_high(HB - 1)
                    for j in range(HP):
                        act.wait_ge(o_done, hh * HP + (j + 1))
                        nc.scalar.activation(o_hi[0:DH, j, :], ps[0:DH, j, 0:HN], ACT.Copy)
                        nc.scalar.activation(o_hi[DH:P, j, :], ps[DH:P, j, HN:2 * HN], ACT.Copy).then_inc(ohi_made, 1)
                split_hi(tile_of(l, 4), SB_, wo_done, l * 4 + 4)
                y_high(l * 8 + 8)
                with act.Fori(0, FI) as i:
                    n0 = l * (FI * FJ) + i * FJ

                    def gelu_of(j):
                        act.wait_ge(gate_done, n0 + (j + 1))
                        nc.scalar.activation(gelu[:, j % 2, :], ps[:, 2 * (j % 2) + 1, :], ACT.Gelu,
                                             bias=gb_s[:, bass.ds((n0 + j) * 2 + 1, 1)]).then_inc(gelu_made, 1)

                    def f_high(j):
                        act.wait_ge(prod_made, n0 + (j + 1))
                        nc.scalar.activation(fT_hi[:, j, :], prod[:, j % 2, :], ACT.Copy).then_inc(fhi_made, 1)

                    split_hi(tile_of(l, 5) + i * 3, SC)
                    gelu_of(0)
                    split_hi(tile_of(l, 6) + i * 3, SA)
                    f_high(0)
                    gelu_of(1)
                    f_high(1)
                    split_hi(tile_of(l, 7) + i * 3, SB_, val_done, n0 + 2)
                    for j in (2, 3):
                        gelu_of(j)
                        f_high(j)

            y_high(8 * L + 4)
            u_high(NC, 4)

        @block.vector
        def _(dve):
            def split_lo(t, slot):
                for k in range(2):
                    dve.wait_ge(whi_made, t * 2 + (k + 1))
                    nc.vector.tensor_tensor(slot_lo[slot][:, k * HT:(k + 1) * HT], w_raw[:, k, :],
                                            slot_hi[slot][:, k * HT:(k + 1) * HT].bitcast(f32), ALU.subtract).then_inc(wlo_made, 1)

            def norm_stats(ln, c, k):
                dve.wait_ge(h_new, ln - NC)
                nc.vector.bn_stats(stats[:, k, :], h[:, c, :]).then_inc(stat_made, 1)
                dve.wait_ge(stat_made, ln)
                alone(dve)
                nc.vector.bn_aggr(mv[:, k, :], stats[:, k, :]).then_inc(mv_made, 1)

            def normed(ln, c, k):
                dve.wait_ge(rstd_made, ln + 1)
                nc.vector.tensor_scalar(xn[:, c, :], h[:, c, :], mv[:, k, 0:1], rstd[:, k:k + 1],
                                        ALU.subtract, ALU.mult).then_inc(xn_made, 1)

            def y_affine(first, wcol, bcol):
                def low(dc):
                    dve.wait_ge(yhi_made, first + (dc + 1))
                    nc.vector.tensor_tensor(y_lo[:, dc, :], y_f[:, dc % 2, :], y_hi[:, dc, :].bitcast(f32),
                                            ALU.subtract).then_inc(ylo_made, 1)
                for dc in range(DC):
                    dve.wait_ge(turned, first + (dc + 1))
                    if dc >= 2:
                        dve.wait_ge(ylo_made, first + (dc - 1))
                    if wcol is None:
                        nc.vector.tensor_copy(y_f[:, dc % 2, :], ps[:, dc, :]).then_inc(yf_made, 1)
                    else:
                        nc.vector.tensor_scalar(y_f[:, dc % 2, :], ps[:, dc, :], wcol(dc), bcol(dc),
                                                ALU.mult, ALU.add).then_inc(yf_made, 1)
                    if dc >= 1:
                        low(dc - 1)
                low(DC - 1)

            def u_low(first, bank):
                for c in range(NC):
                    dve.wait_ge(uhi_made, first + c + 1)
                    nc.vector.scalar_tensor_tensor(u_lo[:, c, :], ps[:, bank + c, :], dinv[:, c:c + 1],
                                                   u_hi[:, c, :].bitcast(f32), ALU.mult, ALU.subtract).then_inc(ulo_made, 1)

            dve.wait_ge(x_in, 16)
            for c in range(NC):
                nc.vector.bn_stats(stats[:, c, :], h[:, c, :]).then_inc(stat_made, 1)
            for c in range(NC):
                dve.wait_ge(stat_made, c + 1)
                nc.vector.bn_aggr(mv[:, c, :], stats[:, c, :]).then_inc(mv_made, 1)
            for c in range(NC):
                dve.wait_ge(rstd_made, c + 1)
                nc.vector.tensor_scalar(xn[:, c, :], h[:, c, :], mv[:, c, 0:1], rstd[:, c:c + 1],
                                        ALU.subtract, ALU.mult).then_inc(pre, 1)
            for c in range(NC):
                dve.wait_ge(pre, c + 1)
                nc.vector.tensor_scalar(xn[:, c, :], xn[:, c, :], 0.0, None, ALU.max).then_inc(xn_made, 1)
            dve.wait_ge(e_in, 32)
            nc.vector.tensor_copy(edge_f[:, :, :], edge_i[:, :, :]).then_inc(pre, 1)
            dve.wait_ge(row_in, 16)
            for c in range(NC):
                to = cn_raw[:, c, :] if c < 2 else ct_raw[:, :, :].rearrange("p a b -> p (a b)")[:, (c - 2) * D:(c - 1) * D]
                nc.vector.tensor_tensor(to, h[:, c, :], y_f[:, 1, :], ALU.add).then_inc(pre, 1)
            for c in range(NC):
                to = cn_raw[:, c, :] if c < 2 else ct_raw[:, :, :].rearrange("p a b -> p (a b)")[:, (c - 2) * D:(c - 1) * D]
                dve.wait_ge(xn_made, c + 1)
                dve.wait_ge(pre, NC + 2 + c)
                nc.vector.tensor_tensor(to, to, xn[:, c, :], ALU.add).then_inc(pre, 1)
            for dc in range(DC):
                dve.wait_ge(turned, dc + 1)
                nc.vector.bn_stats(stats[:, dc, :], ps[:, dc, :]).then_inc(bns, 1)
            for dc in range(DC):
                dve.wait_ge(bns, dc + 1)
                agg = nc.vector.bn_aggr(mv[:, dc, :], stats[:, dc, :])
                agg.then_inc(bns if dc < DC - 1 else mv_made, 1)
            dve.wait_ge(p_in, 48)
            dve.wait_ge(rstd_made, NC + 1)
            nc.vector.tensor_tensor(bn_s[:, :, 0], bn_s[:, :, 0], rstd[:, :], ALU.mult).then_inc(bns, 1)
            dve.wait_ge(bns, 2 * DC)
            nc.vector.tensor_tensor(mv[:, :, 0], mv[:, :, 0], bn_s[:, :, 0], ALU.mult).then_inc(bns, 1)
            dve.wait_ge(bns, 2 * DC + 1)
            nc.vector.tensor_tensor(bn_s[:, :, 1], bn_s[:, :, 1], mv[:, :, 0], ALU.subtract).then_inc(bns, 1)
            dve.wait_ge(bns, 2 * DC + 2)
            y_affine(0, lambda dc: bn_s[:, dc, 0:1], lambda dc: bn_s[:, dc, 1:2])
            split_lo(0, SC)
            split_lo(1, SB_)
            dve.wait_ge(const_made, 9)
            dve.wait_ge(pre, NC + 1)
            with dve.Fori(0, EC // EG) as g:
                for k in range(EG):
                    dve.wait_ge(onehot_free, g * EG + (k + 1))
                    for s in range(2):
                        nc.vector.tensor_scalar(onehot[:, 2 * k + s, :], iota, edge_f[:, s, bass.ds(g * EG + k, 1)], None,
                                                ALU.is_equal).then_inc(onehot_made, 1)
            for c in range(NC):
                dve.wait_ge(adjhi_made, c + 1)
                nc.vector.tensor_tensor(adjl[:, c, :], ps[:, 4 + c, :], adjh[:, c, :].bitcast(f32), ALU.subtract).then_inc(adjlo_made, 1)
            dve.wait_ge(deg_done, 1)
            nc.vector.tensor_copy(deg[:, :], ps[:, 0, 0:2 * NC].rearrange("p (c t) -> p c t", t=2)[:, :, 0]).then_inc(dinv_step, 1)
            dve.wait_ge(dinv_step, 1)
            nc.vector.tensor_scalar(degp[:, :], deg[:, :], 1.0, None, ALU.max).then_inc(dinv_step, 1)
            nc.vector.tensor_scalar(has[:, :], deg[:, :], 0.0, None, ALU.is_gt).then_inc(dinv_step, 1)
            dve.wait_ge(pow_made, 1)
            dve.wait_ge(dinv_step, 3)
            nc.vector.tensor_tensor(dinv[:, :], dinv[:, :], has[:, :], ALU.mult).then_inc(dinv_step, 1)
            dve.wait_ge(dinv_step, 4)
            u_low(0, 0)
            dve.wait_ge(row_in, 32)
            for c in range(NC + 1):
                if c < NC:
                    dve.wait_ge(g_done, c + 1)
                    upd = nc.vector.scalar_tensor_tensor(h[:, c, :], ps[:, 4 + c, :], dinv[:, c:c + 1], bias_row[:, :],
                                                         ALU.mult, ALU.add).then_inc(h_new, 1)
                    norm_stats(NC + 1 + c, c, c)
                if c >= 1:
                    normed(NC + c, c - 1, c - 1)

            with dve.Fori(0, L) as l:
                ln0 = l * 8 + (2 * NC + 1)
                y_affine(l * 8 + 4, lambda dc: ln_s[:, bass.ds(l * 16 + 2 * dc, 1)], lambda dc: ln_s[:, bass.ds(l * 16 + (2 * dc + 1), 1)])
                split_lo(tile_of(l, 1), SC)
                split_lo(tile_of(l, 2), SA)

                def q_low(g, start, count):
                    dve.wait_ge(qhi_made, count)
                    nc.vector.tensor_tensor(q_lo[:, 2 * g:2 * g + 2, :], q_f[:, 2 * g:2 * g + 2, bass.ds(start, HN)],
                                            q_hi[:, 2 * g:2 * g + 2, :].bitcast(f32), ALU.subtract).then_inc(qlo_made, 1)

                for g in range(2):
                    q_low(g, 0, l * 6 + (g + 1))
                split_lo(tile_of(l, 3), SB_)
                with dve.Fori(0, HALVES) as hf:
                    hh = l * 2 + hf
                    nb = hh * HB
                    def ct_low(b):
                        dve.wait_ge(cthi_made, nb + (b + 1))
                        nc.vector.tensor_tensor(ct_lo[:, b % 2, :, :], ct_in_at[b % 2], ct_hi[:, b % 2, :, :].bitcast(f32),
                                                ALU.subtract).then_inc(ctlo_made, 1)

                    def cn_low(b):
                        dve.wait_ge(cnhi_made, nb + (b + 1))
                        nc.vector.tensor_tensor(cn_lo[:, b % 2, :, :], cn_in_at[b % 2], cn_hi[:, b % 2, :, :].bitcast(f32),
                                                ALU.subtract).then_inc(cnlo_made, 1)

                    def row_max(b):
                        dve.wait_ge(s_done, nb + (b + 1))
                        nc.vector.tensor_reduce(nmax[:, b % 2, :], ps[:, b % 2, :].rearrange("p (a m) -> p a m", a=2), AX.X,
                                                ALU.max, negate=True).then_inc(max_made, 1)

                    def inverse(b):
                        dve.wait_ge(exp_made, (nb + (b + 1)) * 2)
                        nc.vector.reciprocal(rsum[:, b % 2, :], esum[:, b % 2, :]).then_inc(rsum_made, 1)

                    def p_low(b):
                        dve.wait_ge(phi_made, nb + (b + 1))
                        nc.vector.tensor_tensor(w_lo[:, :, :], ps[:, 2, :].rearrange("p (a b) -> p a b", a=2),
                                                w_hi[:, :, :].bitcast(f32), ALU.subtract).then_inc(plo_made, 1)

                    def z_low(b):
                        dve.wait_ge(zhi_made, nb + (b + 1))
                        bank = 4 + 2 * (b % 2)
                        nc.vector.tensor_tensor(z_at(1, b), psf[:, bank * 512:(bank + 2) * 512].rearrange("p (d n) -> p d n", n=H * NB),
                                                z_at(0, b).bitcast(f32), ALU.subtract).then_inc(zlo_made, 1)

                    for u in range(UNITS):
                        dve.wait_ge(qkhi_made, hh * UNITS + (u + 1))
                        nc.vector.tensor_tensor(unit_at(1, u), bank_of(u), unit_at(0, u).bitcast(f32), ALU.subtract).then_inc(qklo_made, 1)
                        if u == 1:
                            ct_low(0)
                        if u == 5:
                            ct_low(1)
                        if u == 9:
                            cn_low(0)
                    row_max(0)
                    inverse(0)
                    ct_low(2)
                    row_max(1)
                    inverse(1)
                    for b in range(HB):
                        p_low(b)
                        if b >= 1:
                            z_low(b - 1)
                        if b + 2 < HB:
                            row_max(b + 2)
                        if b + 3 < HB:
                            ct_low(b + 3)
                        if b + 2 < HB:
                            inverse(b + 2)
                        if b + 1 < HB:
                            cn_low(b + 1)
                        if b == HB - 2:
                            for g in range(2):
                                q_low(g, HN - hf * HN, l * 6 + hf * 2 + (g + 3))
                    z_low(HB - 1)
                    for j in range(HP):
                        dve.wait_ge(ohi_made, hh * HP + (j + 1))
                        nc.vector.tensor_tensor(o_lo[0:DH, j, :], ps[0:DH, j, 0:HN], o_hi[0:DH, j, :].bitcast(f32), ALU.subtract)
                        nc.vector.tensor_tensor(o_lo[DH:P, j, :], ps[DH:P, j, HN:2 * HN], o_hi[DH:P, j, :].bitcast(f32),
                                                ALU.subtract).then_inc(olo_made, 1)
                    for c in range(2):
                        at = hf * 2 + c
                        dve.wait_ge(wo_done, hh * 2 + (c + 1))
                        hc = h[:, bass.ds(at, 1), :].rearrange("p a n -> p (a n)")
                        nc.vector.tensor_tensor(hc, hc, ps[:, 4 + c, :], ALU.add).then_inc(h_new, 1)
                        dve.wait_ge(h_new, ln0 - NC + at)
                        alone(dve)
                        nc.vector.bn_stats(stats[:, c, :], hc).then_inc(stat_made, 1)
                        dve.wait_ge(stat_made, ln0 + at)
                        alone(dve)
                        nc.vector.bn_aggr(mv[:, c, :], stats[:, c, :]).then_inc(mv_made, 1)
                    for c in range(2):
                        at = hf * 2 + c
                        hc = h[:, bass.ds(at, 1), :].rearrange("p a n -> p (a n)")
                        dve.wait_ge(rstd_made, ln0 + at + 1)
                        nc.vector.tensor_scalar(xn[:, bass.ds(at, 1), :].rearrange("p a n -> p (a n)"), hc, mv[:, c, 0:1], rstd[:, c:c + 1],
                                                ALU.subtract, ALU.mult).then_inc(xn_made, 1)
                split_lo(tile_of(l, 4), SB_)
                y_affine(l * 8 + 8, lambda dc: ln_s[:, bass.ds(l * 16 + (8 + 2 * dc), 1)], lambda dc: ln_s[:, bass.ds(l * 16 + (9 + 2 * dc), 1)])
                with dve.Fori(0, FI) as i:
                    n0 = l * (FI * FJ) + i * FJ

                    def product(j):
                        dve.wait_ge(gelu_made, n0 + (j + 1))
                        dve.wait_ge(val_done, n0 + (j + 1))
                        if j >= 2:
                            dve.wait_ge(flo_made, n0 + (j - 1))
                        nc.vector.scalar_tensor_tensor(prod[:, j % 2, :], ps[:, 2 * (j % 2), :], gb_s[:, bass.ds((n0 + j) * 2, 1)],
                                                       gelu[:, j % 2, :], ALU.add, ALU.mult).then_inc(prod_made, 1)

                    def f_low(j):
                        dve.wait_ge(fhi_made, n0 + (j + 1))
                        nc.vector.tensor_tensor(fT_lo[:, j, :], prod[:, j % 2, :], fT_hi[:, j, :].bitcast(f32),
                                                ALU.subtract).then_inc(flo_made, 1)

                    split_lo(tile_of(l, 5) + i * 3, SC)
                    product(0)
                    split_lo(tile_of(l, 6) + i * 3, SA)
                    f_low(0)
                    product(1)
                    f_low(1)
                    split_lo(tile_of(l, 7) + i * 3, SB_)
                    for j in (2, 3):
                        product(j)
                        f_low(j)
                    dve.wait_ge(flo_made, n0 + FJ)
                dve.wait_ge(bias_added, l * 4 + 4)
                for c in range(NC + 1):
                    if c < NC:
                        dve.wait_ge(ff_done, l * 16 + (12 + c + 1))
                        nc.vector.tensor_tensor(h[:, c, :], h[:, c, :], ps[:, 4 + c, :], ALU.add).then_inc(h_new, 1)
                        norm_stats(ln0 + (4 + c), c, c)
                    if c >= 1:
                        normed(ln0 + (3 + c), c - 1, c - 1)

            y_affine(8 * L + 4, None, None)
            u_low(NC, 4)
            dve.wait_ge(back_in, 48)
            for c in range(NC):
                dve.wait_ge(g_done, NC + c + 1)
                nc.vector.scalar_tensor_tensor(h[:, c, :], ps[:, c, :], dinv[:, c:c + 1], xn[:, c, :],
                                               ALU.mult, ALU.add).then_inc(h_new, 1)

        @block.tensor
        def _(pe):
            def turn(source, made, first):
                for c in range(NC):
                    pe.wait_ge(made, first(c))
                    for dc in range(DC):
                        tr = nc.tensor.transpose(ps[:, dc, c * P:(c + 1) * P], source[:, c, dc * P:(dc + 1) * P], ident[:, :])
                        if c == NC - 1:
                            tr.then_inc(turned, 1)

            def zero_start(bank):
                for c in range(4):
                    nc.tensor.matmul(ps[:, bank + c, :], zrow[:, 0:P], zrow[:, :], start=True, stop=False, skip_group_check=True)

            def three(bank_ap, pairs, first, last):
                for n, (a, b) in enumerate(pairs):
                    mm = nc.tensor.matmul(bank_ap, a, b, start=first and n == 0, stop=last and n == 2)
                return mm

            def slot(s, w):
                v = (slot_hi if w == 0 else slot_lo)[s]
                return v[:, :].rearrange("p (c n) -> p c n", n=512)

            def gcn(s, tile, bank_u, bank_g, first_y, first_u, adj_wait):
                pe.wait_ge(wlo_made, 2 * (tile + 1))
                for k in range(DC):
                    pe.wait_ge(ylo_made, first_y + k + 1)
                    for c in range(NC):
                        cols = slice(c * P, (c + 1) * P)
                        mm = three(ps[:, bank_u + c, :], split3(y_hi[:, k, cols], y_lo[:, k, cols], slot(s, 0)[:, k, :], slot(s, 1)[:, k, :]),
                                   k == 0, k == DC - 1)
                        if k == DC - 1:
                            mm.then_inc(u_done, 1)
                adj_wait()
                for k in range(NC):
                    pe.wait_ge(ulo_made, first_u + k + 1)
                    for c in range(NC):
                        cols = slice(c * P, (c + 1) * P)
                        mm = three(ps[:, bank_g + c, :], split3(adjh[:, k, cols], adjl[:, k, cols], u_hi[:, k, :], u_lo[:, k, :]),
                                   k == 0, k == NC - 1)
                        if k == NC - 1:
                            mm.then_inc(g_done, 1)

            pe.wait_ge(const_made, 9)
            pe.sem_inc(onehot_free, EG)
            turn(xn, xn_made, lambda c: c + 1)
            zero_start(4)
            with pe.Fori(0, EC // EG) as g:
                for k in range(EG):
                    pe.wait_ge(onehot_made, (g * EG + (k + 1)) * 2)
                    for c in range(NC):
                        mm = nc.tensor.matmul(ps[:, 4 + c, :], onehot[:, 2 * k, c * P:(c + 1) * P], onehot[:, 2 * k + 1, :],
                                              start=False, stop=False, skip_group_check=True)
                    mm.then_inc(onehot_free, 1)
            for c in range(NC):
                nc.tensor.matmul(ps[:, 4 + c, c * P:(c + 1) * P], identb[:, :], identb[:, :], start=False, stop=True,
                                 skip_group_check=True).then_inc(adj_done, 1)
            pe.wait_ge(ylo_made, DC)
            for c in range(NC):
                for k in range(NC):
                    pe.wait_ge(adjlo_made, k + 1)
                    for n, a in enumerate((adjh, adjl)):
                        mm = nc.tensor.matmul(ps[:, 0, 2 * c:2 * c + 2], a[:, k, c * P:(c + 1) * P], ones[:, :],
                                              start=(k == 0 and n == 0), stop=(k == NC - 1 and n == 1))
            mm.then_inc(deg_done, 1)
            pe.wait_ge(dinv_step, 1)
            gcn(SC, 0, 0, 4, 0, 0, lambda: None)

            with pe.Fori(0, L) as l:
                turn(xn, xn_made, lambda c: l * 8 + (4 + c + 1))
                pe.wait_ge(wlo_made, (tile_of(l, 0) + 1) * 2)
                for k in range(DC):
                    pe.wait_ge(ylo_made, l * 8 + (4 + k + 1))
                    for j in range(HP):
                        cols = slice(j * P, (j + 1) * P)
                        mm = three(ps[:, 4 + j, :], split3(slot(SB_, 0)[:, k, cols], slot(SB_, 1)[:, k, cols], y_hi[:, k, :], y_lo[:, k, :]),
                                   k == 0, k == DC - 1)
                        if k == DC - 1:
                            mm.then_inc(q_done, 1)
                with pe.Fori(0, HALVES) as hf:
                    hh = l * 2 + hf
                    nb = hh * HB
                    pe.wait_ge(wlo_made, (tile_of(l, 1) + 1) * 2)
                    for u in range(0, UNITS, 2):
                        dc = u % 8 // 2
                        cols = slice(dc * P, (dc + 1) * P)
                        if u % 8 == 0:
                            pe.wait_ge(qlo_made, l * 6 + hf * 2 + (u // 8 + 1))
                        if u == 4:
                            pe.wait_ge(qf_made, l * HP + HP)
                            pe.wait_ge(h_new, l * 8 + hf * 2 + 4)
                        if u >= 8:
                            pe.wait_ge(qklo_made, hh * UNITS + (u - 6))
                        for jj in range(2):
                            j = u // 8 * 2 + jj
                            for n, (w, q) in enumerate(((0, q_hi), (1, q_hi), (0, q_lo))):
                                for e in range(2):
                                    r = slice(e * DH, (e + 1) * DH)
                                    mm = nc.tensor.matmul(ps[:, (u + e) % 8, jj * HN:(jj + 1) * HN], slot(SC, w)[r, j, cols], q[r, j, :],
                                                          start=n == 0, stop=n == 2)
                                    if jj == 1 and n == 2:
                                        mm.then_inc(qk_done, 1)

                    def scores(b):
                        pe.wait_ge(ctlo_made, nb + (b + 1))
                        if b >= 2:
                            pe.wait_ge(exp_made, (nb + (b - 1)) * 2)
                        for k in range(2):
                            for dc in range(DC):
                                at = (slice(None), dc, slice(k * P, (k + 1) * P))
                                mm = three(ps[:, b % 2, k * M:(k + 1) * M],
                                           split3(z_at(0, b)[at], z_at(1, b)[at], ct_hi[:, b % 2, dc, :], ct_lo[:, b % 2, dc, :]),
                                           dc == 0, dc == DC - 1)
                        mm.then_inc(s_done, 1)

                    def turn_p(b):
                        pe.wait_ge(p_made, nb + (b + 1))
                        for m in range(2):
                            for k in range(2):
                                tr = nc.tensor.transpose(ps[:, 2, m * 2 * P + k * P:m * 2 * P + (k + 1) * P],
                                                         ex[:, b % 2, k, m * P:(m + 1) * P], ident[:, :])
                        tr.then_inc(t_done, 1)

                    def mix(b):
                        pe.wait_ge(plo_made, nb + (b + 1))
                        pe.wait_ge(cnlo_made, nb + (b + 1))
                        if b >= 2:
                            pe.wait_ge(zlo_made, nb + (b - 1))
                        for dc in range(DC):
                            bank = 4 + 2 * (b % 2) + dc // 2
                            for m in range(2):
                                cols = slice(dc * P, (dc + 1) * P)
                                mm = three(ps[:, bank, (dc % 2) * 2 * P:(dc % 2 + 1) * 2 * P],
                                           split3(cn_hi[:, b % 2, m, cols], cn_lo[:, b % 2, m, cols], w_hi[:, m, :], w_lo[:, m, :]),
                                           m == 0, m == 1)
                        mm.then_inc(z_done, 1)

                    pe.wait_ge(qklo_made, (hh + 1) * UNITS)
                    scores(0)
                    scores(1)
                    turn_p(0)
                    for b in range(HB):
                        if b + 2 < HB:
                            scores(b + 2)
                        mix(b)
                        if b + 1 < HB:
                            turn_p(b + 1)
                    pe.wait_ge(wlo_made, (tile_of(l, 2) + 1) * 2)
                    pe.wait_ge(zlo_made, nb + HB)
                    for j in range(HP):
                        for e in range(2):
                            for dc in range(DC):
                                cols = slice(j * P, (j + 1) * P)
                                mm = three(ps[:, j, e * HN:(e + 1) * HN],
                                           split3(slot(SA, 0)[:, dc, cols], slot(SA, 1)[:, dc, cols],
                                                  qz[0][:, dc, :, 2 * j + e, :], qz[1][:, dc, :, 2 * j + e, :]),
                                           dc == 0, dc == DC - 1)
                        mm.then_inc(o_done, 1)
                    pe.wait_ge(wlo_made, (tile_of(l, 3) + 1) * 2)
                    for j in range(HP):
                        pe.wait_ge(olo_made, hh * HP + (j + 1))
                        for c in range(2):
                            cols = slice(c * P, (c + 1) * P)
                            mm = three(ps[:, 4 + c, :], split3(o_hi[:, j, cols], o_lo[:, j, cols], slot(SB_, 0)[:, j, :], slot(SB_, 1)[:, j, :]),
                                       j == 0, j == HP - 1)
                            if j == HP - 1:
                                mm.then_inc(wo_done, 1)
                turn(xn, xn_made, lambda c: l * 8 + (8 + c + 1))
                zero_start(4)
                with pe.Fori(0, FI) as i:
                    n0 = l * (FI * FJ) + i * FJ
                    for j in range(FJ):
                        s = SB_ if j < 2 else SC
                        if j % 2 == 0:
                            pe.wait_ge(wlo_made, (tile_of(l, 4) + j // 2 + i * 3 + 1) * 2)
                        if j >= 2:
                            pe.wait_ge(prod_made, n0 + (j - 1))
                        for vg in (1, 0):
                            for k in range(DC):
                                if j == 0:
                                    pe.wait_ge(ylo_made, l * 8 + (8 + k + 1))
                                cols = slice(vg * 256 + (j % 2) * P, vg * 256 + (j % 2 + 1) * P)
                                mm = three(ps[:, 2 * (j % 2) + vg, :], split3(slot(s, 0)[:, k, cols], slot(s, 1)[:, k, cols], y_hi[:, k, :], y_lo[:, k, :]),
                                           k == 0, k == DC - 1)
                            mm.then_inc(gate_done if vg else val_done, 1)
                    pe.wait_ge(wlo_made, (tile_of(l, 6) + i * 3 + 1) * 2)
                    for j in range(FJ):
                        pe.wait_ge(flo_made, n0 + (j + 1))
                        for c in range(NC):
                            cols = slice(c * P, (c + 1) * P)
                            for n, (a, b) in enumerate(split3(fT_hi[:, j, cols], fT_lo[:, j, cols], slot(SA, 0)[:, j, :], slot(SA, 1)[:, j, :])):
                                mm = nc.tensor.matmul(ps[:, 4 + c, :], a, b, start=False, stop=(j == FJ - 1 and n == 2), skip_group_check=True)
                            if j == FJ - 1:
                                mm.then_inc(ff_done, 1)

            turn(h, h_new, lambda c: 8 * L + 4 - NC + c + 1)
            gcn(SB_, NT - 1, 4, 0, 8 * L + 4, NC, lambda: pe.wait_ge(back_in, 48))


def kernel(**inputs):
    import numpy as np
    import concourse.bacc as bacc
    from concourse.bass_utils import run_bass_kernel_spmd as run

    g = {k.replace("L0_gnn_", ""): np.asarray(v) for k, v in inputs.items()}

    def rows_tile(w):
        return w.reshape(4, P, 512).transpose(1, 0, 2).reshape(P, TILE)

    tiles = [rows_tile(g["gcn_in_w"])]
    for l in range(L):
        tiles += [rows_tile(g["Wq"][l]), rows_tile(g["Wk"][l].T), rows_tile(g["Wv"][l]), rows_tile(g["Wo"][l])]
        gg = g["geglu_w"][l].reshape(DC, P, 2, 2 * FI, 256).transpose(3, 1, 0, 2, 4).reshape(2 * FI, P, TILE)
        ff = g["ffo_w"][l].reshape(FI, FJ, P, D).transpose(0, 2, 1, 3).reshape(FI, P, TILE)
        for i in range(FI):
            tiles += [gg[2 * i], gg[2 * i + 1], ff[i]]
    tiles.append(rows_tile(g["gcn_out_w"]))
    cond = g["cond"]
    arrays = {
        "x": g["x"], "src": g["src"], "dst": g["dst"],
        "tiles": np.stack(tiles),
        "cond_n": cond.reshape(HALVES, HB, 2, P, D).transpose(0, 1, 3, 2, 4).reshape(HALVES, HB, P, 2 * D),
        "cond_t": cond.transpose(0, 2, 1).reshape(HALVES, HB, DC, P, M).transpose(0, 1, 3, 2, 4).reshape(HALVES, HB, P, DC * M),
        "bn_p": np.stack([g["bn_w"].reshape(DC, P).T, g["bn_b"].reshape(DC, P).T], axis=-1),
        "ln_p": np.stack([np.stack([g["ln2_w"], g["ln3_w"]], 1), np.stack([g["ln2_b"], g["ln3_b"]], 1)], -1)
                .reshape(L, 2, DC, P, 2).transpose(3, 0, 1, 2, 4).reshape(P, L * 2 * DC * 2),
        "gb_p": g["geglu_b"].reshape(L, 2, FI, FJ, P).transpose(4, 0, 2, 3, 1).reshape(P, L * FI * FJ * 2),
        "rows": np.concatenate([g["gcn_in_b"][None], g["ffo_b"], g["gcn_out_b"][None]]),
    }
    arrays = {k: np.ascontiguousarray(v) for k, v in arrays.items()}
    nc = bacc.Bacc("TRN2", target_bir_lowering=False, num_devices=1)
    args = [nc.dram_tensor(k, v.shape, mybir.dt.from_np(v.dtype), kind="ExternalInput").ap() for k, v in arrays.items()]
    out = nc.dram_tensor("out", (N, D), mybir.dt.float32, kind="ExternalOutput").ap()
    adj_hi = nc.dram_tensor("adj_hi", (P, NC, N), mybir.dt.float32, kind="Internal").ap()
    adj_lo = nc.dram_tensor("adj_lo", (P, NC, N), mybir.dt.float32, kind="Internal").ap()
    rest = nc.dram_tensor("rest", (P, NC, D), mybir.dt.float32, kind="Internal").ap()
    build(nc, *args, out, adj_hi, adj_lo, rest)
    return run(nc, [arrays], core_ids=[0]).results[0]["out"]
```

```python
import concourse.bass as bass
from concourse import mybir
from contextlib import ExitStack

P = 128
N, D = 512, 512
BS, M = 16, 256
H, DH = 8, 64
L, E = 4, 8192
F = 4 * D
EPS = 1e-5
NB = N // BS
NC = N // P
DC = D // P
HALVES = 2
HN = N // HALVES
HB = BS // HALVES
HP = H // 2
TILE = 2048
HT = TILE // 2
FI = 4
FJ = F // P // FI
LT = 4 + 3 * FI
NT = 2 + L * LT
EC = E // P
EG = 8
EDGE_LOOPS = (0, 2, 5, EC // EG)
UNITS = DC * HP


def build(nc, x, src, dst, tiles, cond_n, cond_t, bn_p, ln_p, gb_p, rows, out, adj_hi, adj_lo, rest):
    f32, f32r = mybir.dt.float32, mybir.dt.float32r
    bf16, f16, i32 = mybir.dt.bfloat16, mybir.dt.float16, mybir.dt.int32
    ALU, ACT, AX = mybir.AluOpType, mybir.ActivationFunctionType, mybir.AxisListType

    ctx = ExitStack()
    with ctx:
        def sb(name, shape, dt):
            return ctx.enter_context(nc.sbuf_tensor(name, shape, dt))

        def sem(name):
            return ctx.enter_context(nc.semaphore(name))

        slot_hi = [sb(f"slot_hi{s}", [P, TILE], f32r) for s in range(3)]
        slot_lo = [sb(f"slot_lo{s}", [P, TILE], f32r) for s in range(3)]
        SA, SB_, SC = 0, 1, 2
        w_raw = sb("w_raw", [P, 2, HT], f32)
        qz_hi = sb("qz_hi", [P, DC * H * HN], f32r)
        qz_lo = sb("qz_lo", [P, DC * H * HN], f32r)
        qz = [t[:, :].rearrange("p (d b h n) -> p d b h n", d=DC, b=HB, h=H) for t in (qz_hi, qz_lo)]
        def part(t, n):
            return t[:, n * TILE:(n + 1) * TILE].rearrange("p (c n) -> p c n", n=512)
        y_hi, y_lo = part(qz_hi, 0), part(qz_lo, 0)
        fT_hi, fT_lo = part(qz_hi, 1), part(qz_lo, 1)
        adjh, adjl = part(qz_hi, 1), part(qz_lo, 1)
        u_hi, u_lo = part(qz_hi, 2), part(qz_lo, 2)
        ct_raw = sb("ct_raw", [P, DC, M], f32)
        cn_raw = sb("cn_raw", [P, 2, D], f32)
        ct_in_at = [ct_raw[:, :, :], w_raw[:, 0, :].rearrange("p (c m) -> p c m", c=DC)]
        cn_in_at = [cn_raw[:, :, :], w_raw[:, 1, :].rearrange("p (c n) -> p c n", c=2)]
        ct_hi = sb("ct_hi", [P, 2, DC, M], f32r)
        ct_lo = sb("ct_lo", [P, 2, DC, M], f32r)
        cn_hi = sb("cn_hi", [P, 2, 2, D], f32r)
        cn_lo = sb("cn_lo", [P, 2, 2, D], f32r)
        q_f = sb("q_f", [P, HP, N], f32)
        whole = [q_f[:, :, :].rearrange("p a n -> p (a n)"), ct_raw[:, :, :].rearrange("p a n -> p (a n)"),
                 cn_raw[:, :, :].rearrange("p a n -> p (a n)")]
        onehot = [t[:, k * D:(k + 1) * D].bitcast(bf16).rearrange("p (s n) -> p s n", s=2)
                  for t in whole for k in range(t.shape[1] // D)]
        gelu = q_f[:, 0:2, :]
        prod = q_f[:, 2:4, :]
        q_hi = sb("q_hi", [P, HP, HN], f32r)
        q_lo = sb("q_lo", [P, HP, HN], f32r)
        o_hi, o_lo = (t[:, 0, :, :].rearrange("p c n -> p (c n)").rearrange("p (j n) -> p j n", j=HP) for t in (cn_hi, cn_lo))
        h = sb("h", [P, NC, D], f32)
        xn = sb("xn", [P, NC, D], f32)
        ex = sb("ex", [P, 2, 2, M], f32)
        y_f = ex[:, :, :, :].rearrange("p a b m -> p a (b m)")
        w_hi = sb("w_hi", [P, 2, 2 * P], f32r)
        w_lo = sb("w_lo", [P, 2, 2 * P], f32r)
        bias_row = sb("bias_row", [P, D], f32)
        iota = bias_row[:, 0:D // 2].bitcast(f16)
        ident = sb("ident", [P, P], f32)
        identb = sb("identb", [P, P], bf16)
        zrow = sb("zrow", [1, D], bf16)
        ones_f = sb("ones_f", [P, 2], f32)
        ones = sb("ones", [P, 2], f32r)
        edge_i = sb("edge_i", [P, 2, EC], i32)
        edge_f = sb("edge_f", [P, 2, EC], f32)
        bn_s = sb("bn_s", [P, DC, 2], f32)
        ln_s = sb("ln_s", [P, L * 2 * DC * 2], f32)
        gb_s = sb("gb_s", [P, L * FI * FJ * 2], f32)
        stats = sb("stats", [P, 4, 6], f32)
        mv = sb("mv", [P, 4, 2], f32)
        vare = sb("vare", [P, 4], f32)
        mhalf = sb("mhalf", [P, 4], f32)
        epsc = sb("epsc", [P, 4], f32)
        rstd = sb("rstd", [P, 4], f32)
        deg = sb("deg", [P, NC], f32)
        degp = sb("degp", [P, NC], f32)
        has = sb("has", [P, NC], f32)
        dinv = sb("dinv", [P, NC], f32)
        nmax = sb("nmax", [P, 2, 2], f32)
        esum = sb("esum", [P, 2, 2], f32)
        rsum = sb("rsum", [P, 2, 2], f32)
        warm = sb("warm", [1, 1], f32)
        zeroc = sb("zeroc", [P, 4], f32)
        nmean = sb("nmean", [P, 4], f32)
        shift = sb("shift", [P, 4], f32)

        ps = ctx.enter_context(nc.psum_tensor("ps", [P, 8, 512], f32))
        psf = ps[:, :, :].rearrange("p b n -> p (b n)")

        x_in, e_in, p_in, row_in = sem("x_in"), sem("e_in"), sem("p_in"), sem("row_in")
        raw_in = [sem("raw_in0"), sem("raw_in1")]
        ct_in, cn_in = [sem("ct_in0"), sem("ct_in1")], [sem("cn_in0"), sem("cn_in1")]
        adj_out, rest_out, back_in, out_done = sem("adj_out"), sem("rest_out"), sem("back_in"), sem("out_done")
        whi_made, wlo_made = sem("whi_made"), sem("wlo_made")
        cthi_made, ctlo_made, cnhi_made, cnlo_made = (sem(n) for n in ("cthi_made", "ctlo_made", "cnhi_made", "cnlo_made"))
        const_made, onehot_made, onehot_free, adj_done = (sem(n) for n in ("const_made", "onehot_made", "onehot_free", "adj_done"))
        adjhi_made, adjlo_made, deg_done, dinv_step, pow_made = (sem(n) for n in ("adjhi_made", "adjlo_made", "deg_done", "dinv_step", "pow_made"))
        u_done, uhi_made, ulo_made, g_done = (sem(n) for n in ("u_done", "uhi_made", "ulo_made", "g_done"))
        passed = sem("passed")
        t_made = sem("t_made")
        edges_made, rest_step = sem("edges_made"), sem("rest_step")
        bns = sem("bns")
        h_new, stat_made, mv_made, rstd_step, rstd_made, xn_made = (sem(n) for n in ("h_new", "stat_made", "mv_made", "rstd_step", "rstd_made", "xn_made"))
        turned, yf_made, yhi_made, ylo_made = (sem(n) for n in ("turned", "yf_made", "yhi_made", "ylo_made"))
        q_done, qf_made, qhi_made, qlo_made = (sem(n) for n in ("q_done", "qf_made", "qhi_made", "qlo_made"))
        qk_done, qkhi_made, qklo_made = (sem(n) for n in ("qk_done", "qkhi_made", "qklo_made"))
        s_done, max_made, exp_made, rsum_made, p_made = (sem(n) for n in ("s_done", "max_made", "exp_made", "rsum_made", "p_made"))
        t_done, phi_made, plo_made = (sem(n) for n in ("t_done", "phi_made", "plo_made"))
        z_done, zhi_made, zlo_made = (sem(n) for n in ("z_done", "zhi_made", "zlo_made"))
        o_done, ohi_made, olo_made, wo_done = (sem(n) for n in ("o_done", "ohi_made", "olo_made", "wo_done"))
        gate_done, val_done, gelu_made, prod_made, fhi_made, flo_made, ff_done = (
            sem(n) for n in ("gate_done", "val_done", "gelu_made", "prod_made", "fhi_made", "flo_made", "ff_done"))

        block = ctx.enter_context(nc.Block())

        def alone(eng):
            eng.sem_inc(passed, 1)

        def tile_of(l, k):
            return l * LT + (1 + k)

        def z_at(w, b):
            return qz[w][:, :, b, :, :].rearrange("p d h n -> p d (h n)")

        def unit_at(w, u):
            dc, first = u % 8 // 2, 4 * (u // 8) + u % 2
            return qz[w][:, dc, :, first:first + 3:2, :].rearrange("p b e n -> p e b n")

        unit_bank = (0, 1, 2, 5, 6, 7, 3, 4)
        o_bank, wo_bank = (0, 1, 2, 5), (3, 4)

        def bank_of(u):
            return ps[:, unit_bank[u % 8], :].rearrange("p (e b n) -> p e b n", e=2, b=HB)

        def s_bank(b, k):
            return 3 if b == 0 and k == 1 else b % 2

        def s_count(hh, b, k=1):
            return hh * (HB + 1) + (b + 1 + (k if b == 0 else 1))

        def z_count(hh, b, last=True):
            return hh * (HB + 1) + (b + 1 + (1 if b == HB - 1 and last else 0))

        def p_at(w, b):
            return (ct_hi, ct_lo)[w][:, 0, 0:2, :] if b == HB - 1 else (w_hi, w_lo)[w][:, :, :]

        def split3(hi_a, lo_a, hi_b, lo_b):
            return ((hi_a, hi_b), (lo_a, hi_b), (hi_a, lo_b))

        @block.sync
        def _(sp):
            def load_tile(t):
                for k in range(2):
                    if not (isinstance(t, int) and t == 0):
                        sp.wait_ge(wlo_made, t * 2 + (k - 1))
                    sp.dma_start(w_raw[:, k, :], tiles[t, :, k * HT:(k + 1) * HT]).then_inc(raw_in[k], 16)

            sp.dma_start(edge_i[:, 0, :], src.rearrange("(p c) -> p c", p=P)).then_inc(e_in, 16)
            sp.dma_start(edge_i[:, 1, :], dst.rearrange("(p c) -> p c", p=P)).then_inc(e_in, 16)
            sp.dma_start(h[:, :, :], x.rearrange("(c p) n -> p c n", p=P)).then_inc(x_in, 16)
            sp.dma_start(y_f[:, 1, :], rows[L + 1:L + 2, :].broadcast_to([P, D])).then_inc(row_in, 16)
            sp.dma_start(bn_s[:, :, :], bn_p).then_inc(p_in, 16)
            load_tile(0)
            sp.dma_start(ln_s[:, :], ln_p).then_inc(p_in, 16)
            sp.dma_start(gb_s[:, :], gb_p).then_inc(p_in, 16)
            sp.wait_ge(rest_step, 2 * NC)
            sp.dma_start(rest, h[:, :, :]).then_inc(rest_out, 16)
            load_tile(1)
            sp.wait_ge(onehot_made, 2 * EC)
            sp.dma_start(bias_row[:, :], rows[0:1, :].broadcast_to([P, D])).then_inc(row_in, 16)
            sp.wait_ge(adjlo_made, NC)
            sp.dma_start(adj_hi, adjh.bitcast(f32)).then_inc(adj_out, 16)
            sp.dma_start(adj_lo, adjl.bitcast(f32)).then_inc(adj_out, 16)
            sp.wait_ge(adj_out, 32)

            load_tile(tile_of(0, 1))

            def load_first(hf):
                sp.dma_start(ct_raw[:, :, :], cond_t[hf, 0, :, :].rearrange("p (c m) -> p c m", c=DC)).then_inc(ct_in[0], 16)
                sp.dma_start(cn_raw[:, :, :], cond_n[hf, 0, :, :].rearrange("p (c n) -> p c n", c=2)).then_inc(cn_in[0], 16)

            load_first(0)
            with sp.Fori(0, L) as l:
                sp.wait_ge(h_new, l * 8 + 4)
                sp.dma_start(bias_row[:, :], rows[l + 1, :].unsqueeze(0).broadcast_to([P, D])).then_inc(row_in, 16)
                for k in (2, 3):
                    load_tile(tile_of(l, k))
                with sp.Fori(0, HALVES) as hf:
                    nb = l * BS + hf * HB

                    def load_ct(b):
                        if b == 1:
                            sp.wait_ge(wlo_made, tile_of(l, 3) * 2 + 1)
                        if b >= 2:
                            sp.wait_ge(ctlo_made, nb + (b - 1))
                        sp.dma_start(ct_in_at[b % 2], cond_t[hf, b, :, :].rearrange("p (c m) -> p c m", c=DC)).then_inc(ct_in[b % 2], 16)

                    def load_cn(b):
                        if b == 1:
                            sp.wait_ge(wlo_made, (tile_of(l, 3) + 1) * 2)
                        if b >= 2:
                            sp.wait_ge(cnlo_made, nb + (b - 1))
                        sp.dma_start(cn_in_at[b % 2], cond_n[hf, b, :, :].rearrange("p (c n) -> p c n", c=2)).then_inc(cn_in[b % 2], 16)

                    load_ct(1)
                    load_cn(1)
                    load_ct(2)
                    for b in range(HB):
                        if b + 3 < HB:
                            load_ct(b + 3)
                        if b + 2 < HB:
                            load_cn(b + 2)
                    sp.wait_ge(ctlo_made, nb + (HB - 1))
                    alone(sp)
                    sp.wait_ge(cnlo_made, nb + (HB - 1))
                    alone(sp)
                    load_first(1 - hf)
                    sp.wait_ge(ctlo_made, nb + HB)
                    alone(sp)
                    sp.wait_ge(cnlo_made, nb + HB)
                    alone(sp)
                load_tile(tile_of(l, 4))
                with sp.Fori(0, FI) as i:
                    for k in (5, 6, 7):
                        load_tile(tile_of(l, k) + i * 3)
                load_tile(tile_of(l, LT + 1))

            sp.wait_ge(ff_done, L * FI * NC)
            sp.dma_start(adjh.bitcast(f32), adj_hi).then_inc(back_in, 16)
            sp.dma_start(adjl.bitcast(f32), adj_lo).then_inc(back_in, 16)
            sp.wait_ge(xn_made, 8 * L + 2 * NC)
            sp.dma_start(xn[:, :, :], rest).then_inc(back_in, 16)
            for c in range(NC):
                sp.wait_ge(h_new, 4 + 8 * L + c + 1)
                sp.dma_start(out.rearrange("(c p) n -> p c n", p=P)[:, c, :], h[:, c, :]).then_inc(out_done, 16)
            sp.wait_ge(out_done, 16 * NC)

        @block.gpsimd
        def _(pool):
            nc.gpsimd.iota(iota, [[1, D]], base=0, channel_multiplier=0,
                           allow_small_or_imprecise_dtypes=True).then_inc(const_made, 1)
            nc.gpsimd.memset(zrow[:, :], 0.0).then_inc(const_made, 1)
            nc.gpsimd.memset(ones_f[:, :], 1.0).then_inc(const_made, 1)
            nc.gpsimd.memset(mhalf[:, :], -0.5).then_inc(const_made, 1)
            nc.gpsimd.memset(epsc[:, :], EPS).then_inc(const_made, 1)
            nc.gpsimd.memset(zeroc[:, :], 0.0)
            nc.gpsimd.memset(ident[:, :], 0.0).then_inc(const_made, 1)
            pool.wait_ge(const_made, 6)
            nc.gpsimd.affine_select(out=ident[:, :], in_=ident[:, :], compare_op=ALU.not_equal, fill=1.0,
                                    base=0, pattern=[[-1, P]], channel_multiplier=1).then_inc(const_made, 1)

            def power(ln, k, steps=1):
                pool.wait_ge(mv_made, ln + 1)
                nc.gpsimd.tensor_tensor(vare[:, k:k + steps], mv[:, k:k + steps, 1], epsc[:, k:k + steps], ALU.add).then_inc(rstd_step, 1)
                pool.wait_ge(rstd_step, ln + 1)
                nc.gpsimd.tensor_tensor(rstd[:, k:k + steps], vare[:, k:k + steps], mhalf[:, k:k + steps], ALU.pow).then_inc(rstd_made, 1)

            def scaling(ln, k):
                step = (ln - (NC + 1)) * 3 + (NC + 1)
                pool.wait_ge(mv_made, ln + 1)
                nc.gpsimd.tensor_tensor(vare[:, k:k + 1], mv[:, k:k + 1, 1], epsc[:, k:k + 1], ALU.add).then_inc(rstd_step, 1)
                nc.gpsimd.tensor_tensor(nmean[:, k:k + 1], zeroc[:, k:k + 1], mv[:, k:k + 1, 0], ALU.subtract).then_inc(rstd_step, 1)
                pool.wait_ge(rstd_step, step + 1)
                nc.gpsimd.tensor_tensor(rstd[:, k:k + 1], vare[:, k:k + 1], mhalf[:, k:k + 1], ALU.pow).then_inc(rstd_step, 1)
                pool.wait_ge(rstd_step, step + 3)
                nc.gpsimd.tensor_tensor(shift[:, k:k + 1], nmean[:, k:k + 1], rstd[:, k:k + 1], ALU.mult).then_inc(rstd_made, 1)

            for c in range(NC):
                power(c, c)
            pool.wait_ge(row_in, 16)
            for c in range(NC):
                pool.wait_ge(t_made, c + 1)
                nc.gpsimd.tensor_tensor(h[:, c, :], h[:, c, :], y_f[:, 1, :], ALU.add).then_inc(rest_step, 1)
            for c in range(NC):
                pool.wait_ge(xn_made, c + 1)
                pool.wait_ge(rest_step, c + 1)
                nc.gpsimd.tensor_tensor(h[:, c, :], h[:, c, :], xn[:, c, :], ALU.add).then_inc(rest_step, 1)
            power(NC, 0, DC)
            pool.wait_ge(dinv_step, 2)
            nc.gpsimd.tensor_tensor(dinv[:, :], degp[:, :], mhalf[:, :], ALU.pow).then_inc(pow_made, 1)
            for c in range(NC):
                scaling(NC + 1 + c, c)
            with pool.Fori(0, L) as l:
                ln0 = l * 8 + (2 * NC + 1)

                def second_half(t, slot):
                    pool.wait_ge(whi_made, t * 2 + 2)
                    pool.wait_ge(wlo_made, t * 2 + 1)
                    nc.gpsimd.tensor_tensor(slot_lo[slot][:, HT:2 * HT], w_raw[:, 1, :],
                                            slot_hi[slot][:, HT:2 * HT].bitcast(f32), ALU.subtract).then_inc(wlo_made, 1)

                second_half(tile_of(l, 3), SB_)
                with pool.Fori(0, HALVES) as hf:
                    hh = l * 2 + hf
                    nb = hh * HB
                    pool.wait_ge(cthi_made, nb + 2)
                    nc.gpsimd.tensor_tensor(ct_lo[:, 1, :, :], ct_in_at[1], ct_hi[:, 1, :, :].bitcast(f32), ALU.subtract).then_inc(ctlo_made, 1)
                    pool.wait_ge(cnhi_made, nb + 1)
                    nc.gpsimd.tensor_tensor(cn_lo[:, 0, :, :], cn_in_at[0], cn_hi[:, 0, :, :].bitcast(f32), ALU.subtract).then_inc(cnlo_made, 1)
                    for k in range(2):
                        pool.wait_ge(rsum_made, s_count(hh, 0, k))
                        nc.gpsimd.tensor_tensor(ex[:, 0, k, :], ex[:, 0, k, :], rsum[:, 0, k:k + 1].broadcast_to([P, M]), ALU.mult).then_inc(p_made, 1)
                    for b in range(1, HB):
                        pool.wait_ge(rsum_made, s_count(hh, b))
                        nc.gpsimd.tensor_tensor(ex[:, b % 2, :, :], ex[:, b % 2, :, :],
                                                rsum[:, b % 2, :].unsqueeze(2).broadcast_to([P, 2, M]), ALU.mult).then_inc(p_made, 1)
                    for c in range(2):
                        scaling(ln0 + (hf * 2 + c), c)
                second_half(tile_of(l, 4), SB_)
                for c in range(NC):
                    scaling(ln0 + (4 + c), c)

        @block.scalar
        def _(act):
            def split_hi(t, slot, used=None, value=0, both=False):
                if both:
                    act.wait_ge(raw_in[1], t * 16 + 16)
                for k in range(2):
                    act.wait_ge(raw_in[k], t * 16 + 16)
                    if k == 0 and used is not None:
                        act.wait_ge(used, value)
                    nc.scalar.activation(slot_hi[slot][:, k * HT:(k + 1) * HT], w_raw[:, k, :], ACT.Copy).then_inc(whi_made, 1)

            def y_high(first):
                for dc in range(DC):
                    act.wait_ge(yf_made, first + (dc + 1))
                    nc.scalar.activation(y_hi[:, dc, :], y_f[:, dc % 2, :], ACT.Copy).then_inc(yhi_made, 1)

            def normed(ln, at, c, source):
                act.wait_ge(rstd_made, ln + 1)
                to = xn[:, c, :] if at is None else xn[:, bass.ds(at, 1), :].rearrange("p a n -> p (a n)")
                nc.scalar.activation(to, source, ACT.Identity, bias=shift[:, c:c + 1], scale=rstd[:, c:c + 1]).then_inc(xn_made, 1)

            def exp_table():
                nc.scalar.activation(warm[:, :], ident[0:1, 0:1], ACT.Exp)

            def u_high(first, bank):
                for c in range(NC):
                    act.wait_ge(u_done, first + c + 1)
                    nc.scalar.activation(u_hi[:, c, :], ps[:, bank + c, :], ACT.Copy, scale=dinv[:, c:c + 1]).then_inc(uhi_made, 1)

            act.wait_ge(const_made, 7)
            nc.scalar.activation(identb[:, :], ident[:, :], ACT.Copy).then_inc(const_made, 1)
            nc.scalar.activation(ones[:, :], ones_f[:, :], ACT.Copy).then_inc(const_made, 1)
            for c in range(NC):
                act.wait_ge(t_made, c + 1)
                nc.scalar.activation(xn[:, c, :], xn[:, c, :], ACT.Relu).then_inc(xn_made, 1)
            split_hi(0, SC)
            y_high(0)
            split_hi(1, SB_)
            for c in range(NC):
                act.wait_ge(adj_done, c + 1)
                nc.scalar.activation(adjh[:, c, :], ps[:, 4 + c, :], ACT.Copy).then_inc(adjhi_made, 1)
            act.wait_ge(dinv_step, 4)
            u_high(0, 0)
            split_hi(tile_of(0, 1), SC)
            act.wait_ge(ct_in[0], 16)
            nc.scalar.activation(ct_hi[:, 0, :, :], ct_raw[:, :, :], ACT.Copy).then_inc(cthi_made, 1)
            for c in range(NC):
                normed(NC + 1 + c, None, c, h[:, c, :])

            exp_table()
            with act.Fori(0, L) as l:
                y_high(l * 8 + 4)
                split_hi(tile_of(l, 2), SA)

                def q_high(g, start, count):
                    act.wait_ge(qf_made, count)
                    nc.scalar.activation(q_hi[:, 2 * g:2 * g + 2, :], q_f[:, 2 * g:2 * g + 2, bass.ds(start, HN)], ACT.Copy).then_inc(qhi_made, 1)

                for j in range(HP):
                    act.wait_ge(q_done, l * HP + (j + 1))
                    nc.scalar.activation(q_f[:, j, :], ps[:, 4 + j, :], ACT.Copy, scale=DH ** -0.5).then_inc(qf_made, 1)
                    if j % 2:
                        q_high(j // 2, 0, l * HP + (j + 1))
                split_hi(tile_of(l, 3), SB_, q_done, l * HP + HP)
                with act.Fori(0, HALVES) as hf:
                    hh = l * 2 + hf
                    nb = hh * HB

                    def ct_high(b):
                        act.wait_ge(ct_in[b % 2], (hh * (HB // 2) + (b // 2 + 1)) * 16)
                        if b == HB:
                            act.wait_ge(z_done, z_count(hh, HB - 1))
                        elif b >= 2:
                            act.wait_ge(s_done, s_count(hh, b - 2))
                        nc.scalar.activation(ct_hi[:, b % 2, :, :], ct_in_at[b % 2], ACT.Copy).then_inc(cthi_made, 1)

                    def cn_high(b):
                        act.wait_ge(cn_in[b % 2], (hh * (HB // 2) + (b // 2 + 1)) * 16)
                        if b >= 2:
                            act.wait_ge(z_done, z_count(hh, b - 2))
                        nc.scalar.activation(cn_hi[:, b % 2, :, :], cn_in_at[b % 2], ACT.Copy).then_inc(cnhi_made, 1)

                    def exps(b, ks=(0, 1)):
                        act.wait_ge(max_made, s_count(hh, b, ks[-1]))
                        for k in ks:
                            nc.scalar.activation(ex[:, b % 2, k, :], ps[:, s_bank(b, k), k * M:(k + 1) * M], ACT.Exp,
                                                 bias=nmax[:, b % 2, k:k + 1], accum_out=esum[:, b % 2, k:k + 1]).then_inc(exp_made, 1)

                    def p_high(b):
                        act.wait_ge(t_done, nb + (b + 1))
                        nc.scalar.activation(p_at(0, b), ps[:, 2, :].rearrange("p (a b) -> p a b", a=2), ACT.Copy).then_inc(phi_made, 1)

                    def z_high(b):
                        if b < HB - 1:
                            act.wait_ge(z_done, z_count(hh, b))
                            bank = 4 + 2 * (b % 2)
                            nc.scalar.activation(z_at(0, b), psf[:, bank * 512:(bank + 2) * 512].rearrange("p (d n) -> p d n", n=H * NB),
                                                 ACT.Copy).then_inc(zhi_made, 1)
                        else:
                            for part in range(2):
                                act.wait_ge(z_done, z_count(hh, b, part == 1))
                                nc.scalar.activation(z_at(0, b)[:, 2 * part:2 * part + 2, :], ps[:, 6 + part, :].rearrange("p (d n) -> p d n", d=2),
                                                     ACT.Copy).then_inc(zhi_made, 1)

                    for u in range(UNITS):
                        act.wait_ge(qk_done, hh * UNITS + (u + 1))
                        nc.scalar.activation(unit_at(0, u), bank_of(u), ACT.Copy).then_inc(qkhi_made, 1)
                        if u == 5:
                            ct_high(1)
                        if u == 9:
                            cn_high(0)
                    exps(0, (0,))
                    exps(0, (1,))
                    ct_high(2)
                    exps(1)
                    for b in range(HB):
                        p_high(b)
                        if b == HB - 1:
                            for g in range(2):
                                q_high(g, HN - hf * HN, l * HP + HP)
                        if b >= 1:
                            z_high(b - 1)
                        if b + 3 < HB:
                            ct_high(b + 3)
                        if b + 1 < HB:
                            cn_high(b + 1)
                        if b + 2 < HB:
                            exps(b + 2)
                    z_high(HB - 1)
                    ct_high(HB)
                    for j in range(HP):
                        act.wait_ge(o_done, hh * HP + (j + 1))
                        nc.scalar.activation(o_hi[0:DH, j, :], ps[0:DH, o_bank[j], 0:HN], ACT.Copy)
                        nc.scalar.activation(o_hi[DH:P, j, :], ps[DH:P, o_bank[j], HN:2 * HN], ACT.Copy).then_inc(ohi_made, 1)
                    for c in range(2):
                        normed(l * 8 + hf * 2 + (2 * NC + 1 + c), hf * 2 + c, c, ps[:, wo_bank[c], :])
                split_hi(tile_of(l, 4), SB_, wo_done, l * 4 + 4, both=True)
                y_high(l * 8 + 8)
                with act.Fori(0, FI) as i:
                    n0 = l * (FI * FJ) + i * FJ

                    def gelu_of(j):
                        act.wait_ge(gate_done, n0 + (j + 1))
                        nc.scalar.activation(gelu[:, j % 2, :], ps[:, 2 * (j % 2) + 1, :], ACT.Gelu,
                                             bias=gb_s[:, bass.ds((n0 + j) * 2 + 1, 1)]).then_inc(gelu_made, 1)

                    def f_high(j):
                        act.wait_ge(prod_made, n0 + (j + 1))
                        nc.scalar.activation(fT_hi[:, j, :], prod[:, j % 2, :], ACT.Copy).then_inc(fhi_made, 1)

                    split_hi(tile_of(l, 5) + i * 3, SC, both=True)
                    gelu_of(0)
                    split_hi(tile_of(l, 6) + i * 3, SA)
                    f_high(0)
                    gelu_of(1)
                    f_high(1)
                    split_hi(tile_of(l, 7) + i * 3, SB_, val_done, n0 + 2)
                    for j in (2, 3):
                        gelu_of(j)
                        f_high(j)
                exp_table()
                split_hi(tile_of(l, LT + 1), SC, val_done, (l + 1) * (FI * FJ))
                for c in range(NC):
                    normed(l * 8 + (2 * NC + 5 + c), None, c, ps[:, 4 + c, :])

            y_high(8 * L + 4)
            u_high(NC, 4)

        @block.vector
        def _(dve):
            def split_lo(t, slot, halves=(0, 1)):
                for k in halves:
                    dve.wait_ge(whi_made, t * 2 + (k + 1))
                    nc.vector.tensor_tensor(slot_lo[slot][:, k * HT:(k + 1) * HT], w_raw[:, k, :],
                                            slot_hi[slot][:, k * HT:(k + 1) * HT].bitcast(f32), ALU.subtract).then_inc(wlo_made, 1)

            def norm_stats(ln, c, source, ready, value):
                dve.wait_ge(ready, value)
                alone(dve)
                nc.vector.bn_stats(stats[:, c, :], source).then_inc(stat_made, 1)

            def norm_mean(ln, c):
                dve.wait_ge(stat_made, ln)
                alone(dve)
                nc.vector.bn_aggr(mv[:, c, :], stats[:, c, :]).then_inc(mv_made, 1)

            def y_affine(first, wcol, bcol):
                def low(dc):
                    dve.wait_ge(yhi_made, first + (dc + 1))
                    nc.vector.tensor_tensor(y_lo[:, dc, :], y_f[:, dc % 2, :], y_hi[:, dc, :].bitcast(f32),
                                            ALU.subtract).then_inc(ylo_made, 1)
                for dc in range(DC):
                    dve.wait_ge(turned, first + (dc + 1))
                    if dc >= 2:
                        dve.wait_ge(ylo_made, first + (dc - 1))
                    if wcol is None:
                        nc.vector.tensor_copy(y_f[:, dc % 2, :], ps[:, dc, :]).then_inc(yf_made, 1)
                    else:
                        nc.vector.tensor_scalar(y_f[:, dc % 2, :], ps[:, dc, :], wcol(dc), bcol(dc),
                                                ALU.mult, ALU.add).then_inc(yf_made, 1)
                    if dc >= 1:
                        low(dc - 1)
                low(DC - 1)

            def u_low(first, bank):
                for c in range(NC):
                    dve.wait_ge(uhi_made, first + c + 1)
                    nc.vector.scalar_tensor_tensor(u_lo[:, c, :], ps[:, bank + c, :], dinv[:, c:c + 1],
                                                   u_hi[:, c, :].bitcast(f32), ALU.mult, ALU.subtract).then_inc(ulo_made, 1)

            def onehots(first, last):
                with dve.Fori(first, last) as g:
                    for k in range(EG):
                        dve.wait_ge(onehot_free, g * EG + (k + 1))
                        for s in range(2):
                            nc.vector.tensor_scalar(onehot[k][:, s, :], iota, edge_f[:, s, bass.ds(g * EG + k, 1)], None,
                                                    ALU.is_equal).then_inc(onehot_made, 1)

            dve.wait_ge(e_in, 32)
            nc.vector.tensor_copy(edge_f[:, :, :], edge_i[:, :, :]).then_inc(edges_made, 1)
            dve.wait_ge(const_made, 1)
            dve.wait_ge(edges_made, 1)
            onehots(*EDGE_LOOPS[0:2])
            dve.wait_ge(x_in, 16)
            for c in range(NC):
                nc.vector.bn_stats(stats[:, c, :], h[:, c, :]).then_inc(stat_made, 1)
            for c in range(NC):
                dve.wait_ge(stat_made, c + 1)
                nc.vector.bn_aggr(mv[:, c, :], stats[:, c, :]).then_inc(mv_made, 1)
            for c in range(NC):
                dve.wait_ge(rstd_made, c + 1)
                nc.vector.tensor_scalar(xn[:, c, :], h[:, c, :], mv[:, c, 0:1], rstd[:, c:c + 1],
                                        ALU.subtract, ALU.mult).then_inc(t_made, 1)
            onehots(*EDGE_LOOPS[1:3])
            for dc in range(DC):
                dve.wait_ge(turned, dc + 1)
                nc.vector.bn_stats(stats[:, dc, :], ps[:, dc, :]).then_inc(bns, 1)
            for dc in range(DC):
                dve.wait_ge(bns, dc + 1)
                agg = nc.vector.bn_aggr(mv[:, dc, :], stats[:, dc, :])
                agg.then_inc(bns if dc < DC - 1 else mv_made, 1)
            split_lo(0, SC)
            dve.wait_ge(p_in, 48)
            dve.wait_ge(rstd_made, NC + 1)
            nc.vector.tensor_tensor(bn_s[:, :, 0], bn_s[:, :, 0], rstd[:, :], ALU.mult).then_inc(bns, 1)
            dve.wait_ge(bns, 2 * DC)
            nc.vector.tensor_tensor(mv[:, :, 0], mv[:, :, 0], bn_s[:, :, 0], ALU.mult).then_inc(bns, 1)
            dve.wait_ge(bns, 2 * DC + 1)
            nc.vector.tensor_tensor(bn_s[:, :, 1], bn_s[:, :, 1], mv[:, :, 0], ALU.subtract).then_inc(bns, 1)
            dve.wait_ge(bns, 2 * DC + 2)
            dve.wait_ge(rest_step, 2 * NC)
            y_affine(0, lambda dc: bn_s[:, dc, 0:1], lambda dc: bn_s[:, dc, 1:2])
            onehots(*EDGE_LOOPS[2:4])
            split_lo(1, SB_)
            for c in range(NC):
                dve.wait_ge(adjhi_made, c + 1)
                nc.vector.tensor_tensor(adjl[:, c, :], ps[:, 4 + c, :], adjh[:, c, :].bitcast(f32), ALU.subtract).then_inc(adjlo_made, 1)
            dve.wait_ge(deg_done, 1)
            nc.vector.tensor_copy(deg[:, :], ps[:, 4, 0:2 * NC].rearrange("p (c t) -> p c t", t=2)[:, :, 0]).then_inc(dinv_step, 1)
            dve.wait_ge(dinv_step, 1)
            nc.vector.tensor_scalar(degp[:, :], deg[:, :], 1.0, None, ALU.max).then_inc(dinv_step, 1)
            nc.vector.tensor_scalar(has[:, :], deg[:, :], 0.0, None, ALU.is_gt).then_inc(dinv_step, 1)
            dve.wait_ge(pow_made, 1)
            dve.wait_ge(dinv_step, 3)
            nc.vector.tensor_tensor(dinv[:, :], dinv[:, :], has[:, :], ALU.mult).then_inc(dinv_step, 1)
            dve.wait_ge(dinv_step, 4)
            u_low(0, 0)
            dve.wait_ge(row_in, 32)
            dve.wait_ge(rest_out, 16)
            split_lo(tile_of(0, 1), SC)
            dve.wait_ge(cthi_made, 1)
            nc.vector.tensor_tensor(ct_lo[:, 0, :, :], ct_raw[:, :, :], ct_hi[:, 0, :, :].bitcast(f32), ALU.subtract).then_inc(ctlo_made, 1)
            for c in range(NC):
                dve.wait_ge(g_done, c + 1)
                nc.vector.scalar_tensor_tensor(h[:, c, :], ps[:, 4 + c, :], dinv[:, c:c + 1], bias_row[:, :],
                                               ALU.mult, ALU.add).then_inc(h_new, 1)
                norm_stats(NC + 1 + c, c, h[:, c, :], h_new, c + 1)
                norm_mean(NC + 1 + c, c)

            with dve.Fori(0, L) as l:
                ln0 = l * 8 + (2 * NC + 1)
                y_affine(l * 8 + 4, lambda dc: ln_s[:, bass.ds(l * 16 + 2 * dc, 1)], lambda dc: ln_s[:, bass.ds(l * 16 + (2 * dc + 1), 1)])
                split_lo(tile_of(l, 2), SA)

                def q_low(g, start, count):
                    dve.wait_ge(qhi_made, count)
                    nc.vector.tensor_tensor(q_lo[:, 2 * g:2 * g + 2, :], q_f[:, 2 * g:2 * g + 2, bass.ds(start, HN)],
                                            q_hi[:, 2 * g:2 * g + 2, :].bitcast(f32), ALU.subtract).then_inc(qlo_made, 1)

                for g in range(2):
                    q_low(g, 0, l * 6 + (g + 1))
                split_lo(tile_of(l, 3), SB_, (0,))
                with dve.Fori(0, HALVES) as hf:
                    hh = l * 2 + hf
                    nb = hh * HB
                    def ct_low(b):
                        dve.wait_ge(cthi_made, nb + (b + 1))
                        if b == 2:
                            dve.wait_ge(ctlo_made, nb + 2)
                        nc.vector.tensor_tensor(ct_lo[:, b % 2, :, :], ct_in_at[b % 2], ct_hi[:, b % 2, :, :].bitcast(f32),
                                                ALU.subtract).then_inc(ctlo_made, 1)

                    def cn_low(b):
                        dve.wait_ge(cnhi_made, nb + (b + 1))
                        if b == 1:
                            dve.wait_ge(cnlo_made, nb + 1)
                        nc.vector.tensor_tensor(cn_lo[:, b % 2, :, :], cn_in_at[b % 2], cn_hi[:, b % 2, :, :].bitcast(f32),
                                                ALU.subtract).then_inc(cnlo_made, 1)

                    def row_max(b):
                        dve.wait_ge(s_done, s_count(hh, b))
                        nc.vector.tensor_reduce(nmax[:, b % 2, :], ps[:, b % 2, :].rearrange("p (a m) -> p a m", a=2), AX.X,
                                                ALU.max, negate=True).then_inc(max_made, 1)

                    def inverse(b):
                        dve.wait_ge(exp_made, (nb + (b + 1)) * 2)
                        nc.vector.reciprocal(rsum[:, b % 2, :], esum[:, b % 2, :]).then_inc(rsum_made, 1)

                    def first_softmax(k):
                        dve.wait_ge(s_done, s_count(hh, 0, k))
                        nc.vector.tensor_reduce(nmax[:, 0, k:k + 1], ps[:, s_bank(0, k), k * M:(k + 1) * M], AX.X,
                                                ALU.max, negate=True).then_inc(max_made, 1)
                        dve.wait_ge(exp_made, nb * 2 + (k + 1))
                        nc.vector.reciprocal(rsum[:, 0, k:k + 1], esum[:, 0, k:k + 1]).then_inc(rsum_made, 1)

                    def p_low(b):
                        dve.wait_ge(phi_made, nb + (b + 1))
                        nc.vector.tensor_tensor(p_at(1, b), ps[:, 2, :].rearrange("p (a b) -> p a b", a=2),
                                                p_at(0, b).bitcast(f32), ALU.subtract).then_inc(plo_made, 1)

                    def z_low(b):
                        if b < HB - 1:
                            dve.wait_ge(zhi_made, z_count(hh, b))
                            bank = 4 + 2 * (b % 2)
                            nc.vector.tensor_tensor(z_at(1, b), psf[:, bank * 512:(bank + 2) * 512].rearrange("p (d n) -> p d n", n=H * NB),
                                                    z_at(0, b).bitcast(f32), ALU.subtract).then_inc(zlo_made, 1)
                        else:
                            for part in range(2):
                                dve.wait_ge(zhi_made, z_count(hh, b, part == 1))
                                at = (slice(None), slice(2 * part, 2 * part + 2), slice(None))
                                nc.vector.tensor_tensor(z_at(1, b)[at], ps[:, 6 + part, :].rearrange("p (d n) -> p d n", d=2),
                                                        z_at(0, b)[at].bitcast(f32), ALU.subtract).then_inc(zlo_made, 1)

                    for u in range(UNITS):
                        dve.wait_ge(qkhi_made, hh * UNITS + (u + 1))
                        nc.vector.tensor_tensor(unit_at(1, u), bank_of(u), unit_at(0, u).bitcast(f32), ALU.subtract).then_inc(qklo_made, 1)
                    first_softmax(0)
                    first_softmax(1)
                    ct_low(2)
                    row_max(1)
                    inverse(1)
                    for b in range(HB):
                        p_low(b)
                        if b == HB - 1:
                            for g in range(2):
                                q_low(g, HN - hf * HN, l * 6 + hf * 2 + (g + 3))
                        if b >= 1:
                            z_low(b - 1)
                        if b + 2 < HB:
                            row_max(b + 2)
                        if b + 3 < HB:
                            ct_low(b + 3)
                        if b + 2 < HB:
                            inverse(b + 2)
                        if b + 1 < HB:
                            cn_low(b + 1)
                    z_low(HB - 1)
                    ct_low(HB)
                    for j in range(HP):
                        dve.wait_ge(ohi_made, hh * HP + (j + 1))
                        nc.vector.tensor_tensor(o_lo[0:DH, j, :], ps[0:DH, o_bank[j], 0:HN], o_hi[0:DH, j, :].bitcast(f32), ALU.subtract)
                        nc.vector.tensor_tensor(o_lo[DH:P, j, :], ps[DH:P, o_bank[j], HN:2 * HN], o_hi[DH:P, j, :].bitcast(f32),
                                                ALU.subtract).then_inc(olo_made, 1)
                    for c in range(2):
                        norm_stats(ln0 + (hf * 2 + c), c, ps[:, wo_bank[c], :], wo_done, hh * 2 + (c + 1))
                        norm_mean(ln0 + (hf * 2 + c), c)
                    for c in range(2):
                        dve.wait_ge(row_in, l * 16 + 48)
                        dve.wait_ge(xn_made, ln0 + (hf * 2 + c))
                        nc.vector.tensor_tensor(h[:, bass.ds(hf * 2 + c, 1), :].rearrange("p a n -> p (a n)"), ps[:, wo_bank[c], :],
                                                bias_row[:, :], ALU.add).then_inc(h_new, 1)
                split_lo(tile_of(l, 4), SB_, (0,))
                y_affine(l * 8 + 8, lambda dc: ln_s[:, bass.ds(l * 16 + (8 + 2 * dc), 1)], lambda dc: ln_s[:, bass.ds(l * 16 + (9 + 2 * dc), 1)])
                with dve.Fori(0, FI) as i:
                    n0 = l * (FI * FJ) + i * FJ

                    def product(j):
                        dve.wait_ge(gelu_made, n0 + (j + 1))
                        dve.wait_ge(val_done, n0 + (j + 1))
                        if j >= 2:
                            dve.wait_ge(flo_made, n0 + (j - 1))
                        nc.vector.scalar_tensor_tensor(prod[:, j % 2, :], ps[:, 2 * (j % 2), :], gb_s[:, bass.ds((n0 + j) * 2, 1)],
                                                       gelu[:, j % 2, :], ALU.add, ALU.mult).then_inc(prod_made, 1)

                    def f_low(j):
                        dve.wait_ge(fhi_made, n0 + (j + 1))
                        nc.vector.tensor_tensor(fT_lo[:, j, :], prod[:, j % 2, :], fT_hi[:, j, :].bitcast(f32),
                                                ALU.subtract).then_inc(flo_made, 1)

                    split_lo(tile_of(l, 5) + i * 3, SC)
                    product(0)
                    split_lo(tile_of(l, 6) + i * 3, SA)
                    f_low(0)
                    product(1)
                    f_low(1)
                    split_lo(tile_of(l, 7) + i * 3, SB_)
                    for j in (2, 3):
                        product(j)
                        f_low(j)
                    dve.wait_ge(flo_made, n0 + FJ)
                split_lo(tile_of(l, LT + 1), SC)

                def to_h(c):
                    dve.wait_ge(xn_made, ln0 + (4 + c))
                    nc.vector.tensor_copy(h[:, c, :], ps[:, 4 + c, :]).then_inc(h_new, 1)

                for c in range(NC):
                    norm_stats(ln0 + (4 + c), c, ps[:, 4 + c, :], ff_done, l * 16 + (12 + c + 1))
                    norm_mean(ln0 + (4 + c), c)
                    if c >= 1:
                        to_h(c - 1)
                to_h(NC - 1)

            y_affine(8 * L + 4, None, None)
            u_low(NC, 4)
            dve.wait_ge(back_in, 48)
            for c in range(NC):
                dve.wait_ge(g_done, NC + c + 1)
                nc.vector.scalar_tensor_tensor(h[:, c, :], ps[:, c, :], dinv[:, c:c + 1], xn[:, c, :],
                                               ALU.mult, ALU.add).then_inc(h_new, 1)

        @block.tensor
        def _(pe):
            def turn_chunk(source, c):
                for dc in range(DC):
                    tr = nc.tensor.transpose(ps[:, dc, c * P:(c + 1) * P], source[:, c, dc * P:(dc + 1) * P], ident[:, :])
                    if c == NC - 1:
                        tr.then_inc(turned, 1)

            def turn(source, made, first):
                for c in range(NC):
                    pe.wait_ge(made, first(c))
                    turn_chunk(source, c)

            def zero_start(bank):
                for c in range(4):
                    nc.tensor.matmul(ps[:, bank + c, :], zrow[:, 0:P], zrow[:, :], start=True, stop=False, skip_group_check=True)

            def add3(bank_ap, pairs, last):
                for n, (a, b) in enumerate(pairs):
                    mm = nc.tensor.matmul(bank_ap, a, b, start=False, stop=last and n == 2, skip_group_check=True)
                return mm

            def three(bank_ap, pairs, first, last):
                for n, (a, b) in enumerate(pairs):
                    mm = nc.tensor.matmul(bank_ap, a, b, start=first and n == 0, stop=last and n == 2)
                return mm

            def slot(s, w):
                v = (slot_hi if w == 0 else slot_lo)[s]
                return v[:, :].rearrange("p (c n) -> p c n", n=512)

            def project(s, tile, bank_u, first_y):
                pe.wait_ge(wlo_made, 2 * (tile + 1))
                for k in range(DC):
                    pe.wait_ge(ylo_made, first_y + k + 1)
                    for c in range(NC):
                        cols = slice(c * P, (c + 1) * P)
                        mm = three(ps[:, bank_u + c, :], split3(y_hi[:, k, cols], y_lo[:, k, cols], slot(s, 0)[:, k, :], slot(s, 1)[:, k, :]),
                                   k == 0, k == DC - 1)
                        if k == DC - 1:
                            mm.then_inc(u_done, 1)

            def spread(bank_g, first_u):
                for k in range(NC):
                    pe.wait_ge(ulo_made, first_u + k + 1)
                    for c in range(NC):
                        cols = slice(c * P, (c + 1) * P)
                        mm = three(ps[:, bank_g + c, :], split3(adjh[:, k, cols], adjl[:, k, cols], u_hi[:, k, :], u_lo[:, k, :]),
                                   k == 0, k == NC - 1)
                        if k == NC - 1:
                            mm.then_inc(g_done, 1)

            pe.wait_ge(const_made, 9)
            pe.sem_inc(onehot_free, EG)
            zero_start(4)

            def count_edges(first, last):
                with pe.Fori(first, last) as g:
                    for k in range(EG):
                        pe.wait_ge(onehot_made, (g * EG + (k + 1)) * 2)
                        for c in range(NC):
                            mm = nc.tensor.matmul(ps[:, 4 + c, :], onehot[k][:, 0, c * P:(c + 1) * P], onehot[k][:, 1, :],
                                                  start=False, stop=False, skip_group_check=True)
                        mm.then_inc(onehot_free, 1)

            count_edges(*EDGE_LOOPS[0:2])
            turn(xn, xn_made, lambda c: c + 1)
            count_edges(*EDGE_LOOPS[1:3])
            pe.wait_ge(yf_made, DC)
            project(SC, 0, 0, 0)
            count_edges(*EDGE_LOOPS[2:4])
            for c in range(NC):
                nc.tensor.matmul(ps[:, 4 + c, c * P:(c + 1) * P], identb[:, :], identb[:, :], start=False, stop=True,
                                 skip_group_check=True).then_inc(adj_done, 1)
            for k in range(NC):
                pe.wait_ge(adjlo_made, k + 1)
                if k == 0:
                    nc.tensor.matmul(ps[:, 4, 0:2 * NC], zrow[:, 0:P], zrow[:, 0:2 * NC], start=True, stop=False, skip_group_check=True)
                for c in range(NC):
                    for n, a in enumerate((adjh, adjl)):
                        mm = nc.tensor.matmul(ps[:, 4, 2 * c:2 * c + 2], a[:, k, c * P:(c + 1) * P], ones[:, :],
                                              start=False, stop=(k == NC - 1 and n == 1), skip_group_check=True)
            mm.then_inc(deg_done, 1)
            pe.wait_ge(dinv_step, 1)
            spread(4, 0)

            with pe.Fori(0, L) as l:
                turn(xn, xn_made, lambda c: l * 8 + (4 + c + 1))
                pe.wait_ge(wlo_made, (tile_of(l, 0) + 1) * 2)
                pe.wait_ge(h_new, l * 8 + 4)
                for first, ks in ((0, (0, 1)), (2, (0, 1)), (0, (2, 3)), (2, (2, 3))):
                    for k in ks:
                        pe.wait_ge(yhi_made, l * 8 + (4 + k + 1))
                        for j in (first, first + 1):
                            for w in range(2):
                                nc.tensor.matmul(ps[:, 4 + j, :], slot(SB_, w)[:, k, j * P:(j + 1) * P], y_hi[:, k, :],
                                                 start=k == 0 and w == 0, stop=False)
                        pe.wait_ge(ylo_made, l * 8 + (4 + k + 1))
                        for j in (first, first + 1):
                            mm = nc.tensor.matmul(ps[:, 4 + j, :], slot(SB_, 0)[:, k, j * P:(j + 1) * P], y_lo[:, k, :],
                                                  start=False, stop=k == DC - 1)
                            if k == DC - 1:
                                mm.then_inc(q_done, 1)
                with pe.Fori(0, HALVES) as hf:
                    hh = l * 2 + hf
                    nb = hh * HB
                    pe.wait_ge(wlo_made, (tile_of(l, 1) + 1) * 2)
                    for u in range(0, UNITS, 2):
                        dc = u % 8 // 2
                        cols = slice(dc * P, (dc + 1) * P)
                        if u % 8 == 0:
                            pe.wait_ge(qlo_made, l * 6 + hf * 2 + (u // 8 + 1))
                        if u == 2:
                            pe.wait_ge(qf_made, l * HP + HP)
                        if u == 6:
                            pe.wait_ge(h_new, l * 8 + hf * 2 + 4)
                        if u >= 8:
                            pe.wait_ge(qklo_made, hh * UNITS + (u - 6))
                        for jj in range(2):
                            j = u // 8 * 2 + jj
                            for n, (w, q) in enumerate(((0, q_hi), (1, q_hi), (0, q_lo))):
                                for e in range(2):
                                    r = slice(e * DH, (e + 1) * DH)
                                    mm = nc.tensor.matmul(ps[:, unit_bank[(u + e) % 8], jj * HN:(jj + 1) * HN], slot(SC, w)[r, j, cols], q[r, j, :],
                                                          start=n == 0, stop=n == 2)
                                    if jj == 1 and n == 2:
                                        mm.then_inc(qk_done, 1)

                    def scores(b, ks=(0, 1)):
                        pe.wait_ge(ctlo_made, nb + (b + 1))
                        if b >= 2:
                            pe.wait_ge(exp_made, (nb + (b - 1)) * 2)
                        for k in ks:
                            for dc in range(DC):
                                at = (slice(None), dc, slice(k * P, (k + 1) * P))
                                mm = three(ps[:, s_bank(b, k), k * M:(k + 1) * M],
                                           split3(z_at(0, b)[at], z_at(1, b)[at], ct_hi[:, b % 2, dc, :], ct_lo[:, b % 2, dc, :]),
                                           dc == 0, dc == DC - 1)
                        if b == 0 or k == 1:
                            mm.then_inc(s_done, 1)

                    def turn_p(b):
                        pe.wait_ge(p_made, s_count(hh, b))
                        for m in range(2):
                            for k in range(2):
                                tr = nc.tensor.transpose(ps[:, 2, m * 2 * P + k * P:m * 2 * P + (k + 1) * P],
                                                         ex[:, b % 2, k, m * P:(m + 1) * P], ident[:, :])
                        tr.then_inc(t_done, 1)

                    def mix(b):
                        pe.wait_ge(plo_made, nb + (b + 1))
                        pe.wait_ge(cnlo_made, nb + (b + 1))
                        if b >= 2:
                            pe.wait_ge(zlo_made, z_count(hh, b - 2))
                        for dc in range(DC):
                            bank = 4 + 2 * (b % 2) + dc // 2
                            for m in range(2):
                                cols = slice(dc * P, (dc + 1) * P)
                                mm = three(ps[:, bank, (dc % 2) * 2 * P:(dc % 2 + 1) * 2 * P],
                                           split3(cn_hi[:, b % 2, m, cols], cn_lo[:, b % 2, m, cols], p_at(0, b)[:, m, :], p_at(1, b)[:, m, :]),
                                           m == 0, m == 1)
                            if dc == DC - 1 or (b == HB - 1 and dc == 1):
                                mm.then_inc(z_done, 1)

                    pe.wait_ge(qklo_made, hh * UNITS + 10)
                    scores(0, (0,))
                    scores(1, (0,))
                    pe.wait_ge(qklo_made, (hh + 1) * UNITS)
                    scores(0, (1,))
                    scores(1, (1,))
                    turn_p(0)
                    def start_with_h(c):
                        nc.tensor.matmul(ps[:, wo_bank[c], :], ident[:, :], h[:, bass.ds(hf * 2 + c, 1), :].rearrange("p a n -> p (a n)"),
                                         start=True, stop=False, skip_group_check=True)

                    for b in range(HB):
                        if b + 2 < HB:
                            scores(b + 2)
                        if b == HB - 2:
                            start_with_h(0)
                            pe.wait_ge(plo_made, nb + (HB - 1))
                            turn_p(HB - 1)
                        mix(b)
                        if b + 1 < HB - 1:
                            turn_p(b + 1)
                    pe.wait_ge(zlo_made, z_count(hh, HB - 2))
                    start_with_h(1)
                    pe.wait_ge(wlo_made, (tile_of(l, 2) + 1) * 2)
                    pe.wait_ge(zlo_made, z_count(hh, HB - 1))
                    for j in range(HP):
                        for e in range(2):
                            for dc in range(DC):
                                cols = slice(j * P, (j + 1) * P)
                                mm = three(ps[:, o_bank[j], e * HN:(e + 1) * HN],
                                           split3(slot(SA, 0)[:, dc, cols], slot(SA, 1)[:, dc, cols],
                                                  qz[0][:, dc, :, 2 * j + e, :], qz[1][:, dc, :, 2 * j + e, :]),
                                           dc == 0, dc == DC - 1)
                        mm.then_inc(o_done, 1)
                    pe.wait_ge(wlo_made, (tile_of(l, 3) + 1) * 2)
                    for c in range(2):
                        cols = slice(c * P, (c + 1) * P)
                        for j in range(HP):
                            pe.wait_ge(olo_made, hh * HP + (j + 1))
                            mm = add3(ps[:, wo_bank[c], :], split3(o_hi[:, j, cols], o_lo[:, j, cols], slot(SB_, 0)[:, j, :], slot(SB_, 1)[:, j, :]),
                                      j == HP - 1)
                        mm.then_inc(wo_done, 1)
                def ff_from_h(c):
                    nc.tensor.matmul(ps[:, 4 + c, :], ident[:, :], h[:, c, :], start=True, stop=False, skip_group_check=True)

                ff_from_h(1)
                pe.wait_ge(h_new, l * 8 + 7)
                for c in range(NC):
                    pe.wait_ge(xn_made, l * 8 + (c + 9))
                    turn_chunk(xn, c)
                    if c == 2:
                        ff_from_h(c)
                pe.wait_ge(h_new, l * 8 + 8)
                ff_from_h(0)
                ff_from_h(3)
                with pe.Fori(0, FI) as i:
                    n0 = l * (FI * FJ) + i * FJ
                    for j in range(FJ):
                        s = SB_ if j < 2 else SC
                        g_tile = tile_of(l, 4) + i * 3 + j // 2
                        if j == 0:
                            pe.wait_ge(wlo_made, g_tile * 2 + 1)
                        if j == 2:
                            pe.wait_ge(wlo_made, g_tile * 2 + 2)
                        if j >= 2:
                            pe.wait_ge(prod_made, n0 + (j - 1))

                        def columns(vg):
                            return slice(vg * 256 + (j % 2) * P, vg * 256 + (j % 2 + 1) * P)

                        if j == 0:
                            pe.wait_ge(yf_made, l * 8 + (8 + 2))
                            for k in range(DC):
                                pe.wait_ge(yhi_made, l * 8 + (8 + k + 1))
                                if k == 2:
                                    pe.wait_ge(wlo_made, g_tile * 2 + 2)
                                for vg in (1, 0):
                                    for w in range(2):
                                        nc.tensor.matmul(ps[:, vg, :], slot(s, w)[:, k, columns(vg)], y_hi[:, k, :],
                                                         start=k == 0 and w == 0, stop=False)
                                pe.wait_ge(ylo_made, l * 8 + (8 + k + 1))
                                for vg in (1, 0):
                                    mm = nc.tensor.matmul(ps[:, vg, :], slot(s, 0)[:, k, columns(vg)], y_lo[:, k, :],
                                                          start=False, stop=k == DC - 1)
                                    if k == DC - 1:
                                        mm.then_inc(gate_done if vg else val_done, 1)
                        else:
                            for vg in (1, 0):
                                for k in range(DC):
                                    mm = three(ps[:, 2 * (j % 2) + vg, :],
                                               split3(slot(s, 0)[:, k, columns(vg)], slot(s, 1)[:, k, columns(vg)], y_hi[:, k, :], y_lo[:, k, :]),
                                               k == 0, k == DC - 1)
                                mm.then_inc(gate_done if vg else val_done, 1)
                    pe.wait_ge(wlo_made, (tile_of(l, 6) + i * 3 + 1) * 2)
                    for j, c in ([(j, c) for j in range(FJ) for c in (0, 1)] + [(j, c) for c in (2, 3) for j in range(FJ)]):
                        pe.wait_ge(flo_made, n0 + (j + 1))
                        cols = slice(c * P, (c + 1) * P)
                        mm = add3(ps[:, 4 + c, :], split3(fT_hi[:, j, cols], fT_lo[:, j, cols], slot(SA, 0)[:, j, :], slot(SA, 1)[:, j, :]),
                                  j == FJ - 1)
                        if j == FJ - 1:
                            mm.then_inc(ff_done, 1)

            turn(h, h_new, lambda c: 8 * L + 4 - NC + c + 1)
            project(SB_, NT - 1, 4, 8 * L + 4)
            pe.wait_ge(back_in, 48)
            spread(0, NC)


def kernel(**inputs):
    import numpy as np
    import concourse.bacc as bacc
    from concourse.bass_utils import run_bass_kernel_spmd as run

    g = {k.replace("L0_gnn_", ""): np.asarray(v) for k, v in inputs.items()}

    def rows_tile(w):
        return w.reshape(4, P, 512).transpose(1, 0, 2).reshape(P, TILE)

    tiles = [rows_tile(g["gcn_in_w"])]
    for l in range(L):
        tiles += [rows_tile(g["Wq"][l]), rows_tile(g["Wk"][l].T), rows_tile(g["Wv"][l]), rows_tile(g["Wo"][l])]
        gg = g["geglu_w"][l].reshape(DC, P, 2, 2 * FI, 256).transpose(3, 1, 0, 2, 4).reshape(2 * FI, P, TILE)
        ff = g["ffo_w"][l].reshape(FI, FJ, P, D).transpose(0, 2, 1, 3).reshape(FI, P, TILE)
        for i in range(FI):
            tiles += [gg[2 * i], gg[2 * i + 1], ff[i]]
    tiles.append(rows_tile(g["gcn_out_w"]))
    tiles.append(tiles[-1])
    cond = g["cond"]
    arrays = {
        "x": g["x"], "src": g["src"], "dst": g["dst"],
        "tiles": np.stack(tiles),
        "cond_n": cond.reshape(HALVES, HB, 2, P, D).transpose(0, 1, 3, 2, 4).reshape(HALVES, HB, P, 2 * D),
        "cond_t": cond.transpose(0, 2, 1).reshape(HALVES, HB, DC, P, M).transpose(0, 1, 3, 2, 4).reshape(HALVES, HB, P, DC * M),
        "bn_p": np.stack([g["bn_w"].reshape(DC, P).T, g["bn_b"].reshape(DC, P).T], axis=-1),
        "ln_p": np.stack([np.stack([g["ln2_w"], g["ln3_w"]], 1), np.stack([g["ln2_b"], g["ln3_b"]], 1)], -1)
                .reshape(L, 2, DC, P, 2).transpose(3, 0, 1, 2, 4).reshape(P, L * 2 * DC * 2),
        "gb_p": g["geglu_b"].reshape(L, 2, FI, FJ, P).transpose(4, 0, 2, 3, 1).reshape(P, L * FI * FJ * 2),
        "rows": np.concatenate([g["gcn_in_b"][None], g["ffo_b"], g["gcn_out_b"][None]]),
    }
    arrays = {k: np.ascontiguousarray(v) for k, v in arrays.items()}
    nc = bacc.Bacc("TRN2", target_bir_lowering=False, num_devices=1)
    args = [nc.dram_tensor(k, v.shape, mybir.dt.from_np(v.dtype), kind="ExternalInput").ap() for k, v in arrays.items()]
    out = nc.dram_tensor("out", (N, D), mybir.dt.float32, kind="ExternalOutput").ap()
    adj_hi = nc.dram_tensor("adj_hi", (P, NC, N), mybir.dt.float32, kind="Internal").ap()
    adj_lo = nc.dram_tensor("adj_lo", (P, NC, N), mybir.dt.float32, kind="Internal").ap()
    rest = nc.dram_tensor("rest", (P, NC, D), mybir.dt.float32, kind="Internal").ap()
    build(nc, *args, out, adj_hi, adj_lo, rest)
    return run(nc, [arrays], core_ids=[0]).results[0]["out"]
```

```python
import concourse.bass as bass
from concourse import mybir
from contextlib import ExitStack

P = 128
N, D = 512, 512
BS, M = 16, 256
H, DH = 8, 64
L, E = 4, 8192
F = 4 * D
EPS = 1e-5
NB = N // BS
NC = N // P
DC = D // P
HALVES = 2
HN = N // HALVES
HB = BS // HALVES
HP = H // 2
TILE = 2048
HT = TILE // 2
FI = 4
FJ = F // P // FI
LT = 4 + 3 * FI
NT = 2 + L * LT
EC = E // P
EG = 8
EDGE_LOOPS = (0, 2, 4, 6, EC // EG)
UNITS = DC * HP


def build(nc, x, src, dst, tiles, cond_n, cond_t, bn_p, ln_p, gb_p, rows, out, adj_hi, adj_lo, rest):
    f32, f32r = mybir.dt.float32, mybir.dt.float32r
    bf16, f16, i32 = mybir.dt.bfloat16, mybir.dt.float16, mybir.dt.int32
    ALU, ACT, AX = mybir.AluOpType, mybir.ActivationFunctionType, mybir.AxisListType

    ctx = ExitStack()
    with ctx:
        def sb(name, shape, dt):
            return ctx.enter_context(nc.sbuf_tensor(name, shape, dt))

        def sem(name):
            return ctx.enter_context(nc.semaphore(name))

        slot_hi = [sb(f"slot_hi{s}", [P, TILE], f32r) for s in range(3)]
        slot_lo = [sb(f"slot_lo{s}", [P, TILE], f32r) for s in range(3)]
        SA, SB_, SC = 0, 1, 2
        w_raw = sb("w_raw", [P, 2, HT], f32)
        qz_hi = sb("qz_hi", [P, DC * H * HN], f32r)
        qz_lo = sb("qz_lo", [P, DC * H * HN], f32r)
        qz = [t[:, :].rearrange("p (d b h n) -> p d b h n", d=DC, b=HB, h=H) for t in (qz_hi, qz_lo)]
        def part(t, n):
            return t[:, n * TILE:(n + 1) * TILE].rearrange("p (c n) -> p c n", n=512)
        y_hi, y_lo = part(qz_hi, 0), part(qz_lo, 0)
        fT_hi, fT_lo = part(qz_hi, 1), part(qz_lo, 1)
        adjh, adjl = part(qz_hi, 1), part(qz_lo, 1)
        u_hi, u_lo = part(qz_hi, 2), part(qz_lo, 2)
        ct_raw = sb("ct_raw", [P, DC, M], f32)
        cn_raw = sb("cn_raw", [P, 2, D], f32)
        ct_in_at = [ct_raw[:, :, :], w_raw[:, 0, :].rearrange("p (c m) -> p c m", c=DC)]
        cn_in_at = [cn_raw[:, :, :], w_raw[:, 1, :].rearrange("p (c n) -> p c n", c=2)]
        ct_hi = sb("ct_hi", [P, 2, DC, M], f32r)
        ct_lo = sb("ct_lo", [P, 2, DC, M], f32r)
        cn_hi = sb("cn_hi", [P, 2, 2, D], f32r)
        cn_lo = sb("cn_lo", [P, 2, 2, D], f32r)
        q_f = sb("q_f", [P, HP, N], f32)
        whole = [q_f[:, :, :].rearrange("p a n -> p (a n)"), ct_raw[:, :, :].rearrange("p a n -> p (a n)"),
                 cn_raw[:, :, :].rearrange("p a n -> p (a n)")]
        onehot = [t[:, k * D:(k + 1) * D].bitcast(bf16).rearrange("p (s n) -> p s n", s=2)
                  for t in whole for k in range(t.shape[1] // D)]
        gelu = q_f[:, 0:2, :]
        prod = q_f[:, 2:4, :]
        q_hi = sb("q_hi", [P, HP, HN], f32r)
        q_lo = sb("q_lo", [P, HP, HN], f32r)
        o_hi, o_lo = (t[:, 0, :, :].rearrange("p c n -> p (c n)").rearrange("p (j n) -> p j n", j=HP) for t in (cn_hi, cn_lo))
        h = sb("h", [P, NC, D], f32)
        xn = sb("xn", [P, NC, D], f32)
        ex = sb("ex", [P, 2, 2, M], f32)
        y_f = ex[:, :, :, :].rearrange("p a b m -> p a (b m)")
        w_hi = sb("w_hi", [P, 2, 2 * P], f32r)
        w_lo = sb("w_lo", [P, 2, 2 * P], f32r)
        bias_row = sb("bias_row", [P, D], f32)
        iota = bias_row[:, 0:D // 2].bitcast(f16)
        ident = sb("ident", [P, P], f32)
        identb = sb("identb", [P, P], bf16)
        zrow = sb("zrow", [1, D], bf16)
        ones_f = sb("ones_f", [P, 2], f32)
        ones = sb("ones", [P, 2], f32r)
        edge_i = sb("edge_i", [P, 2, EC], i32)
        edge_f = sb("edge_f", [P, 2, EC], f32)
        bn_s = sb("bn_s", [P, DC, 2], f32)
        ln_s = sb("ln_s", [P, (L + 1) * 2 * DC * 2], f32)
        gb_s = sb("gb_s", [P, L * FI * FJ * 2], f32)
        stats = sb("stats", [P, 4, 6], f32)
        mv = sb("mv", [P, 4, 2], f32)
        vare = sb("vare", [P, 4], f32)
        mhalf = sb("mhalf", [P, 4], f32)
        epsc = sb("epsc", [P, 4], f32)
        rstd = sb("rstd", [P, 4], f32)
        deg = sb("deg", [P, NC], f32)
        degp = sb("degp", [P, NC], f32)
        has = sb("has", [P, NC], f32)
        dinv = sb("dinv", [P, NC], f32)
        nmax = sb("nmax", [P, 2, 2], f32)
        esum = sb("esum", [P, 2, 2], f32)
        rsum = sb("rsum", [P, 2, 2], f32)
        warm = sb("warm", [1, 1], f32)
        zeroc = sb("zeroc", [P, 4], f32)
        nmean = sb("nmean", [P, 4], f32)
        shift = sb("shift", [P, 4], f32)

        ps = ctx.enter_context(nc.psum_tensor("ps", [P, 8, 512], f32))
        psf = ps[:, :, :].rearrange("p b n -> p (b n)")

        x_in, e_in, p_in, row_in = sem("x_in"), sem("e_in"), sem("p_in"), sem("row_in")
        raw_in = [sem("raw_in0"), sem("raw_in1")]
        ct_in, cn_in = [sem("ct_in0"), sem("ct_in1")], [sem("cn_in0"), sem("cn_in1")]
        adj_out, rest_out, back_in, out_done = sem("adj_out"), sem("rest_out"), sem("back_in"), sem("out_done")
        whi_made, wlo_made, wo_hi_made = sem("whi_made"), sem("wlo_made"), sem("wo_hi_made")
        cthi_made, ctlo_made, cnhi_made, cnlo_made = (sem(n) for n in ("cthi_made", "ctlo_made", "cnhi_made", "cnlo_made"))
        const_made, onehot_made, onehot_free, adj_done = (sem(n) for n in ("const_made", "onehot_made", "onehot_free", "adj_done"))
        adjhi_made, adjlo_made, deg_done, dinv_step, pow_made = (sem(n) for n in ("adjhi_made", "adjlo_made", "deg_done", "dinv_step", "pow_made"))
        deg_row = sem("deg_row")
        u_done, uhi_made, ulo_made, g_done = (sem(n) for n in ("u_done", "uhi_made", "ulo_made", "g_done"))
        passed = sem("passed")
        t_made = sem("t_made")
        edges_made, rest_step = sem("edges_made"), sem("rest_step")
        bns = sem("bns")
        h_new, stat_made, mv_made, rstd_step, rstd_made, xn_made = (sem(n) for n in ("h_new", "stat_made", "mv_made", "rstd_step", "rstd_made", "xn_made"))
        turned, yf_made, yhi_made, ylo_made = (sem(n) for n in ("turned", "yf_made", "yhi_made", "ylo_made"))
        q_done, qf_made, qhi_made, qlo_made = (sem(n) for n in ("q_done", "qf_made", "qhi_made", "qlo_made"))
        qk_done, qkhi_made, qklo_made = (sem(n) for n in ("qk_done", "qkhi_made", "qklo_made"))
        s_done, max_made, exp_made, rsum_made, p_made = (sem(n) for n in ("s_done", "max_made", "exp_made", "rsum_made", "p_made"))
        t_done, phi_made, plo_made = (sem(n) for n in ("t_done", "phi_made", "plo_made"))
        z_done, zhi_made, zlo_made = (sem(n) for n in ("z_done", "zhi_made", "zlo_made"))
        o_done, ohi_made, olo_made, wo_done = (sem(n) for n in ("o_done", "ohi_made", "olo_made", "wo_done"))
        gate_done, val_done, gelu_made, prod_made, fhi_made, flo_made, ff_done = (
            sem(n) for n in ("gate_done", "val_done", "gelu_made", "prod_made", "fhi_made", "flo_made", "ff_done"))

        block = ctx.enter_context(nc.Block())

        def alone(eng):
            eng.sem_inc(passed, 1)

        def tile_of(l, k):
            return l * LT + (1 + k)

        def y_first(l, k):
            return l * 12 + (4 + 4 * k)

        def nodes_of(hf):
            return slice(0, N) if hf is None else slice(hf * HN, (hf + 1) * HN)

        def turned_at(dc, hf):
            return ps[:, dc, :] if hf is None else ps[:, 2 * hf + dc // 2, (dc % 2) * HN:(dc % 2 + 1) * HN]

        def high_of(l, k):
            return l * (LT - 1) + (k if k > 3 else k + 1)

        def z_at(w, b):
            return qz[w][:, :, b, :, :].rearrange("p d h n -> p d (h n)")

        def unit_at(w, u):
            dc, first = u % 8 // 2, 4 * (u // 8) + u % 2
            return qz[w][:, dc, :, first:first + 3:2, :].rearrange("p b e n -> p e b n")

        unit_bank = (0, 1, 2, 5, 6, 7, 3, 4)
        o_bank, wo_bank = (0, 1, 2, 5), (3, 4)

        def bank_of(u):
            return ps[:, unit_bank[u % 8], :].rearrange("p (e b n) -> p e b n", e=2, b=HB)

        def s_bank(b, k):
            return 3 if b == 0 and k == 1 else b % 2

        def s_count(hh, b, k=1):
            return hh * (HB + 1) + (b + 1 + (k if b == 0 else 1))

        def z_count(hh, b, last=True):
            return hh * (HB + 1) + (b + 1 + (1 if b == HB - 1 and last else 0))

        def p_at(w, b):
            return (ct_hi, ct_lo)[w][:, 0, 0:2, :] if b == HB - 1 else (w_hi, w_lo)[w][:, :, :]

        def split3(hi_a, lo_a, hi_b, lo_b):
            return ((hi_a, hi_b), (lo_a, hi_b), (hi_a, lo_b))

        @block.sync
        def _(sp):
            def load_tile(t):
                for k in range(2):
                    if not (isinstance(t, int) and t == 0):
                        sp.wait_ge(wlo_made, t * 2 + (k - 1))
                    sp.dma_start(w_raw[:, k, :], tiles[t, :, k * HT:(k + 1) * HT]).then_inc(raw_in[k], 16)

            sp.dma_start(edge_i[:, 0, :], src.rearrange("(p c) -> p c", p=P)).then_inc(e_in, 16)
            sp.dma_start(edge_i[:, 1, :], dst.rearrange("(p c) -> p c", p=P)).then_inc(e_in, 16)
            sp.dma_start(h[:, :, :], x.rearrange("(c p) n -> p c n", p=P)).then_inc(x_in, 16)
            sp.dma_start(y_f[:, 1, :], rows[L + 1:L + 2, :].broadcast_to([P, D])).then_inc(row_in, 16)
            sp.dma_start(bn_s[:, :, :], bn_p).then_inc(p_in, 16)
            load_tile(0)
            sp.dma_start(ln_s[:, :], ln_p).then_inc(p_in, 16)
            sp.dma_start(gb_s[:, :], gb_p).then_inc(p_in, 16)
            sp.wait_ge(rest_step, 2 * NC)
            sp.dma_start(rest, h[:, :, :]).then_inc(rest_out, 16)
            load_tile(1)
            sp.wait_ge(onehot_made, 2 * EC)
            sp.dma_start(bias_row[:, :], rows[0:1, :].broadcast_to([P, D])).then_inc(row_in, 16)
            sp.wait_ge(adjlo_made, NC)
            sp.dma_start(adj_hi, adjh.bitcast(f32)).then_inc(adj_out, 16)
            sp.dma_start(adj_lo, adjl.bitcast(f32)).then_inc(adj_out, 16)
            sp.wait_ge(adj_out, 32)

            load_tile(tile_of(0, 1))

            def load_first(hf):
                sp.dma_start(ct_raw[:, :, :], cond_t[hf, 0, :, :].rearrange("p (c m) -> p c m", c=DC)).then_inc(ct_in[0], 16)
                sp.dma_start(cn_raw[:, :, :], cond_n[hf, 0, :, :].rearrange("p (c n) -> p c n", c=2)).then_inc(cn_in[0], 16)

            load_first(0)
            with sp.Fori(0, L) as l:
                sp.wait_ge(h_new, l * 8 + 4)
                sp.dma_start(bias_row[:, :], rows[l + 1, :].unsqueeze(0).broadcast_to([P, D])).then_inc(row_in, 16)
                for k in (2, 3):
                    load_tile(tile_of(l, k))
                with sp.Fori(0, HALVES) as hf:
                    nb = l * BS + hf * HB

                    def load_ct(b):
                        if b == 1:
                            sp.wait_ge(wlo_made, tile_of(l, 3) * 2 + 1)
                        if b >= 2:
                            sp.wait_ge(ctlo_made, nb + (b - 1))
                        sp.dma_start(ct_in_at[b % 2], cond_t[hf, b, :, :].rearrange("p (c m) -> p c m", c=DC)).then_inc(ct_in[b % 2], 16)

                    def load_cn(b):
                        if b == 1:
                            sp.wait_ge(wlo_made, (tile_of(l, 3) + 1) * 2)
                        if b >= 2:
                            sp.wait_ge(cnlo_made, nb + (b - 1))
                        sp.dma_start(cn_in_at[b % 2], cond_n[hf, b, :, :].rearrange("p (c n) -> p c n", c=2)).then_inc(cn_in[b % 2], 16)

                    load_ct(1)
                    load_ct(2)
                    load_cn(1)
                    for b in range(HB):
                        if b + 3 < HB:
                            load_ct(b + 3)
                        if b + 2 < HB:
                            load_cn(b + 2)
                    sp.wait_ge(ctlo_made, nb + (HB - 1))
                    alone(sp)
                    sp.wait_ge(cnlo_made, nb + (HB - 1))
                    alone(sp)
                    load_first(1 - hf)
                    sp.wait_ge(ctlo_made, nb + HB)
                    alone(sp)
                    sp.wait_ge(cnlo_made, nb + HB)
                    alone(sp)
                load_tile(tile_of(l, 4))
                with sp.Fori(0, FI) as i:
                    for k in (5, 6, 7):
                        load_tile(tile_of(l, k) + i * 3)
                load_tile(tile_of(l, LT + 1))

            sp.wait_ge(ff_done, L * FI * NC)
            sp.dma_start(adjh.bitcast(f32), adj_hi).then_inc(back_in, 16)
            sp.dma_start(adjl.bitcast(f32), adj_lo).then_inc(back_in, 16)
            sp.wait_ge(xn_made, 8 * L + 2 * NC)
            sp.wait_ge(turned, y_first(L, 1))
            sp.dma_start(xn[:, :, :], rest).then_inc(back_in, 16)
            for c in range(NC):
                sp.wait_ge(h_new, 4 + 8 * L + c + 1)
                sp.dma_start(out.rearrange("(c p) n -> p c n", p=P)[:, c, :], h[:, c, :]).then_inc(out_done, 16)
            sp.wait_ge(out_done, 16 * NC)

        @block.gpsimd
        def _(pool):
            nc.gpsimd.iota(iota, [[1, D]], base=0, channel_multiplier=0,
                           allow_small_or_imprecise_dtypes=True).then_inc(const_made, 1)
            nc.gpsimd.memset(zrow[:, :], 0.0).then_inc(const_made, 1)
            nc.gpsimd.memset(ones_f[:, :], 1.0).then_inc(const_made, 1)
            nc.gpsimd.memset(mhalf[:, :], -0.5).then_inc(const_made, 1)
            nc.gpsimd.memset(epsc[:, :], EPS).then_inc(const_made, 1)
            nc.gpsimd.memset(zeroc[:, :], 0.0)
            nc.gpsimd.memset(ident[:, :], 0.0).then_inc(const_made, 1)
            pool.wait_ge(const_made, 6)
            nc.gpsimd.affine_select(out=ident[:, :], in_=ident[:, :], compare_op=ALU.not_equal, fill=1.0,
                                    base=0, pattern=[[-1, P]], channel_multiplier=1).then_inc(const_made, 1)

            def power(ln, k, steps=1):
                pool.wait_ge(mv_made, ln + 1)
                nc.gpsimd.tensor_tensor(vare[:, k:k + steps], mv[:, k:k + steps, 1], epsc[:, k:k + steps], ALU.add).then_inc(rstd_step, 1)
                pool.wait_ge(rstd_step, ln + 1)
                nc.gpsimd.tensor_tensor(rstd[:, k:k + steps], vare[:, k:k + steps], mhalf[:, k:k + steps], ALU.pow).then_inc(rstd_made, 1)

            def scaling(ln, k):
                step = (ln - (NC + 1)) * 3 + (NC + 1)
                pool.wait_ge(mv_made, ln + 1)
                nc.gpsimd.tensor_tensor(vare[:, k:k + 1], mv[:, k:k + 1, 1], epsc[:, k:k + 1], ALU.add).then_inc(rstd_step, 1)
                nc.gpsimd.tensor_tensor(nmean[:, k:k + 1], zeroc[:, k:k + 1], mv[:, k:k + 1, 0], ALU.subtract).then_inc(rstd_step, 1)
                pool.wait_ge(rstd_step, step + 1)
                nc.gpsimd.tensor_tensor(rstd[:, k:k + 1], vare[:, k:k + 1], mhalf[:, k:k + 1], ALU.pow).then_inc(rstd_step, 1)
                pool.wait_ge(rstd_step, step + 3)
                nc.gpsimd.tensor_tensor(shift[:, k:k + 1], nmean[:, k:k + 1], rstd[:, k:k + 1], ALU.mult).then_inc(rstd_made, 1)

            for c in range(NC):
                power(c, c)
            pool.wait_ge(row_in, 16)
            for c in range(NC):
                pool.wait_ge(t_made, c + 1)
                nc.gpsimd.tensor_tensor(h[:, c, :], h[:, c, :], y_f[:, 1, :], ALU.add).then_inc(rest_step, 1)
            for c in range(NC):
                pool.wait_ge(xn_made, c + 1)
                pool.wait_ge(rest_step, c + 1)
                nc.gpsimd.tensor_tensor(h[:, c, :], h[:, c, :], xn[:, c, :], ALU.add).then_inc(rest_step, 1)
            power(NC, 0, DC)
            pool.wait_ge(dinv_step, 2)
            nc.gpsimd.tensor_tensor(dinv[:, :], degp[:, :], mhalf[:, :], ALU.pow).then_inc(pow_made, 1)

            def second_half(l, k, slot):
                t = tile_of(l, k)
                pool.wait_ge(whi_made, high_of(l, k) * 2 + 2)
                pool.wait_ge(wlo_made, t * 2 + 1)
                nc.gpsimd.tensor_tensor(slot_lo[slot][:, HT:2 * HT], w_raw[:, 1, :],
                                        slot_hi[slot][:, HT:2 * HT].bitcast(f32), ALU.subtract).then_inc(wlo_made, 1)

            second_half(0, 1, SC)
            for c in range(NC):
                scaling(NC + 1 + c, c)
            with pool.Fori(0, L) as l:
                ln0 = l * 8 + (2 * NC + 1)

                wo_tile = tile_of(l, 3)
                pool.wait_ge(q_done, l * HP + HP)
                pool.wait_ge(wlo_made, wo_tile * 2)
                pool.wait_ge(raw_in[1], wo_tile * 16 + 16)
                pool.wait_ge(raw_in[0], wo_tile * 16 + 16)
                for k in range(2):
                    cols = slice(k * HT, (k + 1) * HT)
                    nc.gpsimd.tensor_tensor(slot_hi[SB_][:, cols], w_raw[:, k, :], zeroc[:, 0:1].broadcast_to([P, HT]), ALU.add).then_inc(wo_hi_made, 1)
                    pool.wait_ge(wo_hi_made, l * 2 + (k + 1))
                    nc.gpsimd.tensor_tensor(slot_lo[SB_][:, cols], w_raw[:, k, :], slot_hi[SB_][:, cols].bitcast(f32), ALU.subtract).then_inc(wlo_made, 1)
                with pool.Fori(0, HALVES) as hf:
                    hh = l * 2 + hf
                    nb = hh * HB
                    pool.wait_ge(cnhi_made, nb + 1)
                    nc.gpsimd.tensor_tensor(cn_lo[:, 0, :, :], cn_in_at[0], cn_hi[:, 0, :, :].bitcast(f32), ALU.subtract).then_inc(cnlo_made, 1)
                    for k in range(2):
                        pool.wait_ge(rsum_made, s_count(hh, 0, k))
                        nc.gpsimd.tensor_tensor(ex[:, 0, k, :], ex[:, 0, k, :], rsum[:, 0, k:k + 1].broadcast_to([P, M]), ALU.mult).then_inc(p_made, 1)
                    for b in range(1, HB):
                        pool.wait_ge(rsum_made, s_count(hh, b))
                        nc.gpsimd.tensor_tensor(ex[:, b % 2, :, :], ex[:, b % 2, :, :],
                                                rsum[:, b % 2, :].unsqueeze(2).broadcast_to([P, 2, M]), ALU.mult).then_inc(p_made, 1)
                    for c in range(2):
                        scaling(ln0 + (hf * 2 + c), c)
                second_half(l, 4, SB_)
                for c in range(NC):
                    scaling(ln0 + (4 + c), c)
                    if c == 1:
                        second_half(l, LT + 1, SC)

        @block.scalar
        def _(act):
            def split_hi(t, slot, used=None, value=0, both=False):
                if both:
                    act.wait_ge(raw_in[1], t * 16 + 16)
                for k in range(2):
                    act.wait_ge(raw_in[k], t * 16 + 16)
                    if k == 0 and used is not None:
                        act.wait_ge(used, value)
                    nc.scalar.activation(slot_hi[slot][:, k * HT:(k + 1) * HT], w_raw[:, k, :], ACT.Copy).then_inc(whi_made, 1)

            def y_high(first, hf=None, chunks=range(DC)):
                at = nodes_of(hf)
                for dc in chunks:
                    act.wait_ge(yf_made, first + (dc + 1))
                    nc.scalar.activation(y_hi[:, dc, at], y_f[:, dc % 2, 0:at.stop - at.start], ACT.Copy).then_inc(yhi_made, 1)

            def normed(ln, at, c, source):
                act.wait_ge(rstd_made, ln + 1)
                to = xn[:, c, :] if at is None else xn[:, bass.ds(at, 1), :].rearrange("p a n -> p (a n)")
                nc.scalar.activation(to, source, ACT.Identity, bias=shift[:, c:c + 1], scale=rstd[:, c:c + 1]).then_inc(xn_made, 1)

            def exp_table():
                nc.scalar.activation(warm[:, :], ident[0:1, 0:1], ACT.Exp)

            def u_high(first, bank):
                for c in range(NC):
                    act.wait_ge(u_done, first + c + 1)
                    nc.scalar.activation(u_hi[:, c, :], ps[:, bank + c, :], ACT.Copy, scale=dinv[:, c:c + 1]).then_inc(uhi_made, 1)

            act.wait_ge(const_made, 7)
            nc.scalar.activation(identb[:, :], ident[:, :], ACT.Copy).then_inc(const_made, 1)
            nc.scalar.activation(ones[:, :], ones_f[:, :], ACT.Copy).then_inc(const_made, 1)
            for c in range(NC):
                act.wait_ge(t_made, c + 1)
                nc.scalar.activation(xn[:, c, :], xn[:, c, :], ACT.Relu).then_inc(xn_made, 1)
            split_hi(0, SC)
            y_high(0)
            split_hi(1, SB_)
            for c in range(NC):
                act.wait_ge(adj_done, c + 1)
                nc.scalar.activation(adjh[:, c, :], ps[:, 4 + c, :], ACT.Copy).then_inc(adjhi_made, 1)
            act.wait_ge(dinv_step, 4)
            u_high(0, 0)
            split_hi(tile_of(0, 1), SC)
            act.wait_ge(ct_in[0], 16)
            nc.scalar.activation(ct_hi[:, 0, :, :], ct_raw[:, :, :], ACT.Copy).then_inc(cthi_made, 1)
            for c in range(NC):
                normed(NC + 1 + c, None, c, h[:, c, :])
            exp_table()
            y_high(y_first(0, 0), 0)
            with act.Fori(0, L) as l:
                y_high(y_first(l, 1), 1)

                def q_high(g, start, count):
                    act.wait_ge(qf_made, count)
                    nc.scalar.activation(q_hi[:, 2 * g:2 * g + 2, :], q_f[:, 2 * g:2 * g + 2, bass.ds(start, HN)], ACT.Copy).then_inc(qhi_made, 1)

                for half in range(HALVES):
                    for g in range(2):
                        act.wait_ge(q_done, l * HP + (2 * half + g + 1))
                        nc.scalar.activation(q_f[:, 2 * g:2 * g + 2, nodes_of(half)], ps[:, 4 + 2 * half + g, :].rearrange("p (j n) -> p j n", j=2),
                                             ACT.Copy, scale=DH ** -0.5).then_inc(qf_made, 1)
                    if half == 0:
                        for g in range(2):
                            q_high(g, 0, l * HP + (g + 1))
                        split_hi(tile_of(l, 2), SA, both=True)
                with act.Fori(0, HALVES) as hf:
                    hh = l * 2 + hf
                    nb = hh * HB

                    def ct_high(b):
                        act.wait_ge(ct_in[b % 2], (hh * (HB // 2) + (b // 2 + 1)) * 16)
                        if b == HB:
                            act.wait_ge(z_done, z_count(hh, HB - 1))
                        elif b >= 2:
                            act.wait_ge(s_done, s_count(hh, b - 2))
                        nc.scalar.activation(ct_hi[:, b % 2, :, :], ct_in_at[b % 2], ACT.Copy).then_inc(cthi_made, 1)

                    def cn_high(b):
                        act.wait_ge(cn_in[b % 2], (hh * (HB // 2) + (b // 2 + 1)) * 16)
                        if b >= 2:
                            act.wait_ge(z_done, z_count(hh, b - 2))
                        nc.scalar.activation(cn_hi[:, b % 2, :, :], cn_in_at[b % 2], ACT.Copy).then_inc(cnhi_made, 1)

                    def exps(b, ks=(0, 1)):
                        act.wait_ge(max_made, s_count(hh, b, ks[-1]))
                        for k in ks:
                            nc.scalar.activation(ex[:, b % 2, k, :], ps[:, s_bank(b, k), k * M:(k + 1) * M], ACT.Exp,
                                                 bias=nmax[:, b % 2, k:k + 1], accum_out=esum[:, b % 2, k:k + 1]).then_inc(exp_made, 1)

                    def p_high(b):
                        act.wait_ge(t_done, nb + (b + 1))
                        nc.scalar.activation(p_at(0, b), ps[:, 2, :].rearrange("p (a b) -> p a b", a=2), ACT.Copy).then_inc(phi_made, 1)

                    def z_high(b):
                        if b < HB - 1:
                            act.wait_ge(z_done, z_count(hh, b))
                            bank = 4 + 2 * (b % 2)
                            nc.scalar.activation(z_at(0, b), psf[:, bank * 512:(bank + 2) * 512].rearrange("p (d n) -> p d n", n=H * NB),
                                                 ACT.Copy).then_inc(zhi_made, 1)
                        else:
                            for part in range(2):
                                act.wait_ge(z_done, z_count(hh, b, part == 1))
                                nc.scalar.activation(z_at(0, b)[:, 2 * part:2 * part + 2, :], ps[:, 6 + part, :].rearrange("p (d n) -> p d n", d=2),
                                                     ACT.Copy).then_inc(zhi_made, 1)

                    for u in range(UNITS):
                        act.wait_ge(qk_done, hh * UNITS + (u + 1))
                        nc.scalar.activation(unit_at(0, u), bank_of(u), ACT.Copy).then_inc(qkhi_made, 1)
                        if u == UNITS - 1:
                            ct_high(1)
                        if u == 9:
                            cn_high(0)
                    exps(0, (0,))
                    ct_high(2)
                    exps(0, (1,))
                    exps(1)
                    for b in range(HB):
                        p_high(b)
                        if b == HB - 1:
                            for g in range(2):
                                q_high(g, HN - hf * HN, l * HP + HP)
                        if b >= 1:
                            z_high(b - 1)
                        if b + 3 < HB:
                            ct_high(b + 3)
                        if b + 1 < HB:
                            cn_high(b + 1)
                        if b + 2 < HB:
                            exps(b + 2)
                    z_high(HB - 1)
                    ct_high(HB)
                    for j in range(HP):
                        act.wait_ge(o_done, hh * HP + (j + 1))
                        nc.scalar.activation(o_hi[0:DH, j, :], ps[0:DH, o_bank[j], 0:HN], ACT.Copy)
                        nc.scalar.activation(o_hi[DH:P, j, :], ps[DH:P, o_bank[j], HN:2 * HN], ACT.Copy).then_inc(ohi_made, 1)
                    for c in range(2):
                        normed(l * 8 + hf * 2 + (2 * NC + 1 + c), hf * 2 + c, c, ps[:, wo_bank[c], :])
                split_hi(tile_of(l, 4), SB_, wo_done, l * 4 + 4, both=True)
                y_high(y_first(l, 2))
                with act.Fori(0, FI) as i:
                    n0 = l * (FI * FJ) + i * FJ

                    def gelu_of(j):
                        act.wait_ge(gate_done, n0 + (j + 1))
                        nc.scalar.activation(gelu[:, j % 2, :], ps[:, 2 * (j % 2) + 1, :], ACT.Gelu,
                                             bias=gb_s[:, bass.ds((n0 + j) * 2 + 1, 1)]).then_inc(gelu_made, 1)

                    def f_high(j):
                        act.wait_ge(prod_made, n0 + (j + 1))
                        nc.scalar.activation(fT_hi[:, j, :], prod[:, j % 2, :], ACT.Copy).then_inc(fhi_made, 1)

                    split_hi(tile_of(l, 5) + i * 3, SC, both=True)
                    gelu_of(0)
                    split_hi(tile_of(l, 6) + i * 3, SA)
                    f_high(0)
                    gelu_of(1)
                    f_high(1)
                    split_hi(tile_of(l, 7) + i * 3, SB_, val_done, n0 + 2)
                    for j in (2, 3):
                        gelu_of(j)
                        f_high(j)
                exp_table()
                split_hi(tile_of(l, LT + 1), SC, val_done, (l + 1) * (FI * FJ))
                for c in range(NC):
                    normed(l * 8 + (2 * NC + 5 + c), None, c, ps[:, 4 + c, :])
                    if c == 2:
                        y_high(y_first(l + 1, 0), 0, (0, 1))
                act.wait_ge(h_new, l * 8 + 10)
                for c in (2, 3):
                    nc.scalar.activation(h[:, c, :], ps[:, 4 + c, :], ACT.Copy).then_inc(h_new, 1)
                y_high(y_first(l + 1, 0), 0, (2, 3))

            y_high(y_first(L, 1))
            u_high(NC, 4)

        @block.vector
        def _(dve):
            def split_lo(high, slot, halves=(0, 1)):
                for k in halves:
                    dve.wait_ge(whi_made, high * 2 + (k + 1))
                    nc.vector.tensor_tensor(slot_lo[slot][:, k * HT:(k + 1) * HT], w_raw[:, k, :],
                                            slot_hi[slot][:, k * HT:(k + 1) * HT].bitcast(f32), ALU.subtract).then_inc(wlo_made, 1)

            def norm_stats(ln, c, source, ready, value):
                dve.wait_ge(ready, value)
                alone(dve)
                nc.vector.bn_stats(stats[:, c, :], source).then_inc(stat_made, 1)

            def norm_mean(ln, c):
                dve.wait_ge(stat_made, ln)
                alone(dve)
                nc.vector.bn_aggr(mv[:, c, :], stats[:, c, :]).then_inc(mv_made, 1)

            def y_affine(first, wcol, bcol, hf=None):
                at = nodes_of(hf)
                width = slice(0, at.stop - at.start)

                def low(dc):
                    dve.wait_ge(yhi_made, first + (dc + 1))
                    nc.vector.tensor_tensor(y_lo[:, dc, at], y_f[:, dc % 2, width], y_hi[:, dc, at].bitcast(f32),
                                            ALU.subtract).then_inc(ylo_made, 1)
                for dc in range(DC):
                    dve.wait_ge(turned, first + (dc + 1 if hf is None else dc // 2 * 2 + 2))
                    if dc >= 2:
                        dve.wait_ge(ylo_made, first + (dc - 1))
                    elif hf == 1:
                        dve.wait_ge(ylo_made, first)
                    if wcol is None:
                        nc.vector.tensor_copy(y_f[:, dc % 2, width], turned_at(dc, hf)).then_inc(yf_made, 1)
                    else:
                        nc.vector.tensor_scalar(y_f[:, dc % 2, width], turned_at(dc, hf), wcol(dc), bcol(dc),
                                                ALU.mult, ALU.add).then_inc(yf_made, 1)
                    if dc >= 1:
                        low(dc - 1)
                low(DC - 1)

            def y_layer(l, k, hf):
                column = (l * 2 + (1 if k == 2 else 0)) * (2 * DC)
                y_affine(y_first(l, k), lambda dc: ln_s[:, bass.ds(column + 2 * dc, 1)],
                         lambda dc: ln_s[:, bass.ds(column + (2 * dc + 1), 1)], hf)

            def u_low(first, bank):
                for c in range(NC):
                    dve.wait_ge(uhi_made, first + c + 1)
                    nc.vector.scalar_tensor_tensor(u_lo[:, c, :], ps[:, bank + c, :], dinv[:, c:c + 1],
                                                   u_hi[:, c, :].bitcast(f32), ALU.mult, ALU.subtract).then_inc(ulo_made, 1)

            def onehots(first, last):
                with dve.Fori(first, last) as g:
                    for k in range(EG):
                        dve.wait_ge(onehot_free, g * EG + (k + 1))
                        for s in range(2):
                            nc.vector.tensor_scalar(onehot[k][:, s, :], iota, edge_f[:, s, bass.ds(g * EG + k, 1)], None,
                                                    ALU.is_equal).then_inc(onehot_made, 1)

            dve.wait_ge(e_in, 32)
            nc.vector.tensor_copy(edge_f[:, :, :], edge_i[:, :, :]).then_inc(edges_made, 1)
            dve.wait_ge(const_made, 1)
            dve.wait_ge(edges_made, 1)
            onehots(*EDGE_LOOPS[0:2])
            dve.wait_ge(x_in, 16)
            for c in range(NC):
                nc.vector.bn_stats(stats[:, c, :], h[:, c, :]).then_inc(stat_made, 1)
            for c in range(NC):
                dve.wait_ge(stat_made, c + 1)
                nc.vector.bn_aggr(mv[:, c, :], stats[:, c, :]).then_inc(mv_made, 1)
            for c in range(NC):
                dve.wait_ge(rstd_made, c + 1)
                nc.vector.tensor_scalar(xn[:, c, :], h[:, c, :], mv[:, c, 0:1], rstd[:, c:c + 1],
                                        ALU.subtract, ALU.mult).then_inc(t_made, 1)
            onehots(*EDGE_LOOPS[1:3])
            for dc in range(DC):
                dve.wait_ge(turned, dc + 1)
                nc.vector.bn_stats(stats[:, dc, :], ps[:, dc, :]).then_inc(bns, 1)
            for dc in range(DC):
                dve.wait_ge(bns, dc + 1)
                agg = nc.vector.bn_aggr(mv[:, dc, :], stats[:, dc, :])
                agg.then_inc(bns if dc < DC - 1 else mv_made, 1)
            onehots(*EDGE_LOOPS[2:4])
            dve.wait_ge(p_in, 48)
            dve.wait_ge(rstd_made, NC + 1)
            nc.vector.tensor_tensor(bn_s[:, :, 0], bn_s[:, :, 0], rstd[:, :], ALU.mult).then_inc(bns, 1)
            dve.wait_ge(bns, 2 * DC)
            nc.vector.tensor_tensor(mv[:, :, 0], mv[:, :, 0], bn_s[:, :, 0], ALU.mult).then_inc(bns, 1)
            dve.wait_ge(bns, 2 * DC + 1)
            nc.vector.tensor_tensor(bn_s[:, :, 1], bn_s[:, :, 1], mv[:, :, 0], ALU.subtract).then_inc(bns, 1)
            dve.wait_ge(bns, 2 * DC + 2)
            dve.wait_ge(rest_step, 2 * NC)
            y_affine(0, lambda dc: bn_s[:, dc, 0:1], lambda dc: bn_s[:, dc, 1:2])
            onehots(*EDGE_LOOPS[3:5])
            split_lo(0, SC)
            split_lo(1, SB_)
            for c in range(NC):
                dve.wait_ge(adjhi_made, c + 1)
                nc.vector.tensor_tensor(adjl[:, c, :], ps[:, 4 + c, :], adjh[:, c, :].bitcast(f32), ALU.subtract).then_inc(adjlo_made, 1)
            dve.wait_ge(deg_done, 1)
            nc.vector.tensor_copy(y_f[0:1, 0, :], ps[0:1, 4, :]).then_inc(deg_row, 1)
            dve.wait_ge(deg_done, 2)
            nc.vector.tensor_copy(deg[:, :], ps[:, 4, 0:NC]).then_inc(dinv_step, 1)
            dve.wait_ge(dinv_step, 1)
            nc.vector.tensor_scalar(degp[:, :], deg[:, :], 1.0, None, ALU.max).then_inc(dinv_step, 1)
            nc.vector.tensor_scalar(has[:, :], deg[:, :], 0.0, None, ALU.is_gt).then_inc(dinv_step, 1)
            dve.wait_ge(pow_made, 1)
            dve.wait_ge(dinv_step, 3)
            nc.vector.tensor_tensor(dinv[:, :], dinv[:, :], has[:, :], ALU.mult).then_inc(dinv_step, 1)
            dve.wait_ge(dinv_step, 4)
            u_low(0, 0)
            dve.wait_ge(row_in, 32)
            dve.wait_ge(rest_out, 16)
            split_lo(high_of(0, 1), SC, (0,))

            def gcn_out_of(c):
                dve.wait_ge(g_done, c + 1)
                nc.vector.scalar_tensor_tensor(h[:, c, :], ps[:, 4 + c, :], dinv[:, c:c + 1], bias_row[:, :],
                                               ALU.mult, ALU.add).then_inc(h_new, 1)

            gcn_out_of(0)
            for c in range(NC):
                norm_stats(NC + 1 + c, c, h[:, c, :], h_new, c + 1)
                if c + 1 < NC:
                    gcn_out_of(c + 1)
                norm_mean(NC + 1 + c, c)
                if c == 1:
                    dve.wait_ge(cthi_made, 1)
                    nc.vector.tensor_tensor(ct_lo[:, 0, :, :], ct_raw[:, :, :], ct_hi[:, 0, :, :].bitcast(f32), ALU.subtract).then_inc(ctlo_made, 1)
            y_layer(0, 0, 0)

            with dve.Fori(0, L) as l:
                ln0 = l * 8 + (2 * NC + 1)
                y_layer(l, 1, 1)

                def q_low(g, start, count):
                    dve.wait_ge(qhi_made, count)
                    nc.vector.tensor_tensor(q_lo[:, 2 * g:2 * g + 2, :], q_f[:, 2 * g:2 * g + 2, bass.ds(start, HN)],
                                            q_hi[:, 2 * g:2 * g + 2, :].bitcast(f32), ALU.subtract).then_inc(qlo_made, 1)

                for g in range(2):
                    q_low(g, 0, l * 6 + (g + 1))
                split_lo(high_of(l, 2), SA)
                with dve.Fori(0, HALVES) as hf:
                    hh = l * 2 + hf
                    nb = hh * HB
                    def ct_low(b):
                        dve.wait_ge(cthi_made, nb + (b + 1))
                        nc.vector.tensor_tensor(ct_lo[:, b % 2, :, :], ct_in_at[b % 2], ct_hi[:, b % 2, :, :].bitcast(f32),
                                                ALU.subtract).then_inc(ctlo_made, 1)

                    def cn_low(b):
                        dve.wait_ge(cnhi_made, nb + (b + 1))
                        if b == 1:
                            dve.wait_ge(cnlo_made, nb + 1)
                        nc.vector.tensor_tensor(cn_lo[:, b % 2, :, :], cn_in_at[b % 2], cn_hi[:, b % 2, :, :].bitcast(f32),
                                                ALU.subtract).then_inc(cnlo_made, 1)

                    def row_max(b):
                        dve.wait_ge(s_done, s_count(hh, b))
                        nc.vector.tensor_reduce(nmax[:, b % 2, :], ps[:, b % 2, :].rearrange("p (a m) -> p a m", a=2), AX.X,
                                                ALU.max, negate=True).then_inc(max_made, 1)

                    def inverse(b):
                        dve.wait_ge(exp_made, (nb + (b + 1)) * 2)
                        nc.vector.reciprocal(rsum[:, b % 2, :], esum[:, b % 2, :]).then_inc(rsum_made, 1)

                    def first_softmax(k):
                        dve.wait_ge(s_done, s_count(hh, 0, k))
                        nc.vector.tensor_reduce(nmax[:, 0, k:k + 1], ps[:, s_bank(0, k), k * M:(k + 1) * M], AX.X,
                                                ALU.max, negate=True).then_inc(max_made, 1)
                        dve.wait_ge(exp_made, nb * 2 + (k + 1))
                        nc.vector.reciprocal(rsum[:, 0, k:k + 1], esum[:, 0, k:k + 1]).then_inc(rsum_made, 1)

                    def p_low(b):
                        dve.wait_ge(phi_made, nb + (b + 1))
                        nc.vector.tensor_tensor(p_at(1, b), ps[:, 2, :].rearrange("p (a b) -> p a b", a=2),
                                                p_at(0, b).bitcast(f32), ALU.subtract).then_inc(plo_made, 1)

                    def z_low(b):
                        if b < HB - 1:
                            dve.wait_ge(zhi_made, z_count(hh, b))
                            bank = 4 + 2 * (b % 2)
                            nc.vector.tensor_tensor(z_at(1, b), psf[:, bank * 512:(bank + 2) * 512].rearrange("p (d n) -> p d n", n=H * NB),
                                                    z_at(0, b).bitcast(f32), ALU.subtract).then_inc(zlo_made, 1)
                        else:
                            for part in range(2):
                                dve.wait_ge(zhi_made, z_count(hh, b, part == 1))
                                at = (slice(None), slice(2 * part, 2 * part + 2), slice(None))
                                nc.vector.tensor_tensor(z_at(1, b)[at], ps[:, 6 + part, :].rearrange("p (d n) -> p d n", d=2),
                                                        z_at(0, b)[at].bitcast(f32), ALU.subtract).then_inc(zlo_made, 1)

                    for u in range(UNITS):
                        dve.wait_ge(qkhi_made, hh * UNITS + (u + 1))
                        nc.vector.tensor_tensor(unit_at(1, u), bank_of(u), unit_at(0, u).bitcast(f32), ALU.subtract).then_inc(qklo_made, 1)
                        if u == UNITS - 1:
                            ct_low(1)
                    first_softmax(0)
                    first_softmax(1)
                    ct_low(2)
                    row_max(1)
                    inverse(1)
                    for b in range(HB):
                        p_low(b)
                        if b == HB - 1:
                            for g in range(2):
                                q_low(g, HN - hf * HN, l * 6 + hf * 2 + (g + 3))
                        if b >= 1:
                            z_low(b - 1)
                        if b + 2 < HB:
                            row_max(b + 2)
                        if b + 3 < HB:
                            ct_low(b + 3)
                        if b + 2 < HB:
                            inverse(b + 2)
                        if b + 1 < HB:
                            cn_low(b + 1)
                    z_low(HB - 1)
                    ct_low(HB)
                    for j in range(HP):
                        dve.wait_ge(ohi_made, hh * HP + (j + 1))
                        nc.vector.tensor_tensor(o_lo[0:DH, j, :], ps[0:DH, o_bank[j], 0:HN], o_hi[0:DH, j, :].bitcast(f32), ALU.subtract)
                        nc.vector.tensor_tensor(o_lo[DH:P, j, :], ps[DH:P, o_bank[j], HN:2 * HN], o_hi[DH:P, j, :].bitcast(f32),
                                                ALU.subtract).then_inc(olo_made, 1)
                    for c in range(2):
                        norm_stats(ln0 + (hf * 2 + c), c, ps[:, wo_bank[c], :], wo_done, hh * 2 + (c + 1))
                        norm_mean(ln0 + (hf * 2 + c), c)
                    for c in range(2):
                        dve.wait_ge(row_in, l * 16 + 48)
                        dve.wait_ge(xn_made, ln0 + (hf * 2 + c))
                        nc.vector.tensor_tensor(h[:, bass.ds(hf * 2 + c, 1), :].rearrange("p a n -> p (a n)"), ps[:, wo_bank[c], :],
                                                bias_row[:, :], ALU.add).then_inc(h_new, 1)
                split_lo(high_of(l, 4), SB_, (0,))
                y_layer(l, 2, None)
                with dve.Fori(0, FI) as i:
                    n0 = l * (FI * FJ) + i * FJ

                    def product(j):
                        dve.wait_ge(gelu_made, n0 + (j + 1))
                        dve.wait_ge(val_done, n0 + (j + 1))
                        if j >= 2:
                            dve.wait_ge(flo_made, n0 + (j - 1))
                        nc.vector.scalar_tensor_tensor(prod[:, j % 2, :], ps[:, 2 * (j % 2), :], gb_s[:, bass.ds((n0 + j) * 2, 1)],
                                                       gelu[:, j % 2, :], ALU.add, ALU.mult).then_inc(prod_made, 1)

                    def f_low(j):
                        dve.wait_ge(fhi_made, n0 + (j + 1))
                        nc.vector.tensor_tensor(fT_lo[:, j, :], prod[:, j % 2, :], fT_hi[:, j, :].bitcast(f32),
                                                ALU.subtract).then_inc(flo_made, 1)

                    split_lo(high_of(l, 5) + i * 3, SC)
                    product(0)
                    split_lo(high_of(l, 6) + i * 3, SA)
                    f_low(0)
                    product(1)
                    f_low(1)
                    split_lo(high_of(l, 7) + i * 3, SB_)
                    for j in (2, 3):
                        product(j)
                        f_low(j)
                    dve.wait_ge(flo_made, n0 + FJ)
                split_lo(high_of(l, LT + 1), SC, (0,))

                for c in range(NC):
                    norm_stats(ln0 + (4 + c), c, ps[:, 4 + c, :], ff_done, l * 16 + (12 + c + 1))
                    norm_mean(ln0 + (4 + c), c)
                    if c == 2:
                        for k in range(2):
                            dve.wait_ge(xn_made, ln0 + (4 + k))
                            nc.vector.tensor_copy(h[:, k, :], ps[:, 4 + k, :]).then_inc(h_new, 1)
                y_layer(l + 1, 0, 0)

            dve.wait_ge(ylo_made, y_first(L, 1))
            y_affine(y_first(L, 1), None, None)
            u_low(NC, 4)
            dve.wait_ge(back_in, 48)
            for c in range(NC):
                dve.wait_ge(g_done, NC + c + 1)
                nc.vector.scalar_tensor_tensor(h[:, c, :], ps[:, c, :], dinv[:, c:c + 1], xn[:, c, :],
                                               ALU.mult, ALU.add).then_inc(h_new, 1)

        @block.tensor
        def _(pe):
            def turn_chunk(source, c):
                for dc in range(DC):
                    tr = nc.tensor.transpose(ps[:, dc, c * P:(c + 1) * P], source[:, c, dc * P:(dc + 1) * P], ident[:, :])
                    if c == NC - 1:
                        tr.then_inc(turned, 1)

            def turn_half(l, half):
                for c in (2 * half, 2 * half + 1):
                    pe.wait_ge(xn_made, l * 8 + (4 + c + 1))
                    for dc in range(DC):
                        tr = nc.tensor.transpose(turned_at(dc, half)[:, (c % 2) * P:(c % 2 + 1) * P], xn[:, c, dc * P:(dc + 1) * P], ident[:, :])
                        if c % 2:
                            tr.then_inc(turned, 1)

            def start_layer(l):
                pe.wait_ge(h_new, l * 8 + 2)
                turn_half(l, 0)
                for bank in (4, 5):
                    nc.tensor.matmul(ps[:, bank, :], zrow[:, 0:P], zrow[:, :], start=True, stop=False, skip_group_check=True)

            def turn(source, made, first):
                for c in range(NC):
                    pe.wait_ge(made, first(c))
                    turn_chunk(source, c)

            def zero_start(bank):
                for c in range(4):
                    nc.tensor.matmul(ps[:, bank + c, :], zrow[:, 0:P], zrow[:, :], start=True, stop=False, skip_group_check=True)

            def add3(bank_ap, pairs, last):
                for n, (a, b) in enumerate(pairs):
                    mm = nc.tensor.matmul(bank_ap, a, b, start=False, stop=last and n == 2, skip_group_check=True)
                return mm

            def three(bank_ap, pairs, first, last):
                for n, (a, b) in enumerate(pairs):
                    mm = nc.tensor.matmul(bank_ap, a, b, start=first and n == 0, stop=last and n == 2)
                return mm

            def slot(s, w):
                v = (slot_hi if w == 0 else slot_lo)[s]
                return v[:, :].rearrange("p (c n) -> p c n", n=512)

            def project(s, tile, bank_u, first_y, chunks=range(DC)):
                pe.wait_ge(wlo_made, 2 * (tile + 1))
                for k in chunks:
                    pe.wait_ge(ylo_made, first_y + k + 1)
                    for c in range(NC):
                        cols = slice(c * P, (c + 1) * P)
                        mm = three(ps[:, bank_u + c, :], split3(y_hi[:, k, cols], y_lo[:, k, cols], slot(s, 0)[:, k, :], slot(s, 1)[:, k, :]),
                                   k == 0, k == DC - 1)
                        if k == DC - 1:
                            mm.then_inc(u_done, 1)

            def spread(bank_g, first_u):
                for k, c in ([(k, c) for k in range(NC) for c in (0, 1)] + [(k, c) for c in (2, 3) for k in range(NC)]):
                    pe.wait_ge(ulo_made, first_u + k + 1)
                    cols = slice(c * P, (c + 1) * P)
                    mm = three(ps[:, bank_g + c, :], split3(adjh[:, k, cols], adjl[:, k, cols], u_hi[:, k, :], u_lo[:, k, :]),
                               k == 0, k == NC - 1)
                    if k == NC - 1:
                        mm.then_inc(g_done, 1)

            pe.wait_ge(const_made, 9)
            pe.sem_inc(onehot_free, EG)
            zero_start(4)

            def count_edges(first, last):
                with pe.Fori(first, last) as g:
                    for k in range(EG):
                        pe.wait_ge(onehot_made, (g * EG + (k + 1)) * 2)
                        for c in range(NC):
                            mm = nc.tensor.matmul(ps[:, 4 + c, :], onehot[k][:, 0, c * P:(c + 1) * P], onehot[k][:, 1, :],
                                                  start=False, stop=False, skip_group_check=True)
                        mm.then_inc(onehot_free, 1)

            count_edges(*EDGE_LOOPS[0:2])
            turn(xn, xn_made, lambda c: c + 1)
            count_edges(EDGE_LOOPS[1], EDGE_LOOPS[-1])
            for c in range(NC):
                nc.tensor.matmul(ps[:, 4 + c, c * P:(c + 1) * P], identb[:, :], identb[:, :], start=False, stop=True,
                                 skip_group_check=True).then_inc(adj_done, 1)
            pe.wait_ge(yf_made, DC)
            project(SC, 0, 0, 0, (0, 1))
            for k in range(NC):
                pe.wait_ge(adjlo_made, k + 1)
                for n, a in enumerate((adjh, adjl)):
                    mm = nc.tensor.matmul(ps[0:2, 4, :], ones[:, :], a[:, k, :], start=k == 0 and n == 0, stop=k == NC - 1 and n == 1)
            mm.then_inc(deg_done, 1)
            project(SC, 0, 0, 0, (2,))
            pe.wait_ge(deg_row, 1)
            for c in range(NC):
                tr = nc.tensor.transpose(ps[:, 4, c:c + 1], y_f[0:1, 0, c * P:(c + 1) * P], ident[0:1, 0:1])
            tr.then_inc(deg_done, 1)
            project(SC, 0, 0, 0, (3,))
            pe.wait_ge(dinv_step, 1)
            spread(4, 0)
            start_layer(0)

            with pe.Fori(0, L) as l:
                pe.wait_ge(wlo_made, (tile_of(l, 0) + 1) * 2)

                def q_product(half, j, k, w, part, start, stop):
                    return nc.tensor.matmul(ps[:, 4 + 2 * half + j // 2, (j % 2) * HN:(j % 2 + 1) * HN], slot(SB_, w)[:, k, j * P:(j + 1) * P],
                                            part[:, k, nodes_of(half)], start=start, stop=stop, skip_group_check=True)

                for k in range(DC):
                    pe.wait_ge(yhi_made, y_first(l, 0) + (k + 1))
                    for j in range(HP):
                        for w in range(2):
                            q_product(0, j, k, w, y_hi, False, False)
                    pe.wait_ge(ylo_made, y_first(l, 0) + (k + 1))
                    for j in range(HP):
                        mm = q_product(0, j, k, 0, y_lo, False, k == DC - 1)
                        if k == DC - 1 and j % 2:
                            mm.then_inc(q_done, 1)
                    if k == 0:
                        turn_half(l, 1)
                pe.wait_ge(h_new, l * 8 + 4)
                for j in range(HP):
                    for k in range(DC):
                        pe.wait_ge(ylo_made, y_first(l, 1) + (k + 1))
                        q_product(1, j, k, 0, y_hi, k == 0, False)
                        q_product(1, j, k, 1, y_hi, False, False)
                        mm = q_product(1, j, k, 0, y_lo, False, k == DC - 1)
                    if j % 2:
                        mm.then_inc(q_done, 1)
                with pe.Fori(0, HALVES) as hf:
                    hh = l * 2 + hf
                    nb = hh * HB
                    pe.wait_ge(wlo_made, tile_of(l, 1) * 2 + 1)
                    for u in range(0, UNITS, 2):
                        dc = u % 8 // 2
                        cols = slice(dc * P, (dc + 1) * P)
                        if u % 8 == 0:
                            pe.wait_ge(qlo_made, l * 6 + hf * 2 + (u // 8 + 1))
                        if u in (2, 4):
                            pe.wait_ge(qf_made, l * HP + u)
                        if u == 6:
                            pe.wait_ge(h_new, l * 8 + hf * 2 + 4)
                        if u == 8:
                            pe.wait_ge(wlo_made, tile_of(l, 1) * 2 + 2)
                        if u >= 8:
                            pe.wait_ge(qklo_made, hh * UNITS + (u - 6))
                        for jj in range(2):
                            j = u // 8 * 2 + jj
                            for n, (w, q) in enumerate(((0, q_hi), (1, q_hi), (0, q_lo))):
                                for e in range(2):
                                    r = slice(e * DH, (e + 1) * DH)
                                    mm = nc.tensor.matmul(ps[:, unit_bank[(u + e) % 8], jj * HN:(jj + 1) * HN], slot(SC, w)[r, j, cols], q[r, j, :],
                                                          start=n == 0, stop=n == 2)
                                    if jj == 1 and n == 2:
                                        mm.then_inc(qk_done, 1)

                    def scores(b, ks=(0, 1)):
                        pe.wait_ge(ctlo_made, nb + (b + 1))
                        if b >= 2:
                            pe.wait_ge(exp_made, (nb + (b - 1)) * 2)
                        for k in ks:
                            for dc in range(DC):
                                at = (slice(None), dc, slice(k * P, (k + 1) * P))
                                mm = three(ps[:, s_bank(b, k), k * M:(k + 1) * M],
                                           split3(z_at(0, b)[at], z_at(1, b)[at], ct_hi[:, b % 2, dc, :], ct_lo[:, b % 2, dc, :]),
                                           dc == 0, dc == DC - 1)
                        if b == 0 or k == 1:
                            mm.then_inc(s_done, 1)

                    def turn_p(b):
                        pe.wait_ge(p_made, s_count(hh, b))
                        for m in range(2):
                            for k in range(2):
                                tr = nc.tensor.transpose(ps[:, 2, m * 2 * P + k * P:m * 2 * P + (k + 1) * P],
                                                         ex[:, b % 2, k, m * P:(m + 1) * P], ident[:, :])
                        tr.then_inc(t_done, 1)

                    def mix(b):
                        pe.wait_ge(plo_made, nb + (b + 1))
                        pe.wait_ge(cnlo_made, nb + (b + 1))
                        if b >= 2:
                            pe.wait_ge(zlo_made, z_count(hh, b - 2))
                        for dc in range(DC):
                            bank = 4 + 2 * (b % 2) + dc // 2
                            for m in range(2):
                                cols = slice(dc * P, (dc + 1) * P)
                                mm = three(ps[:, bank, (dc % 2) * 2 * P:(dc % 2 + 1) * 2 * P],
                                           split3(cn_hi[:, b % 2, m, cols], cn_lo[:, b % 2, m, cols], p_at(0, b)[:, m, :], p_at(1, b)[:, m, :]),
                                           m == 0, m == 1)
                            if dc == DC - 1 or (b == HB - 1 and dc == 1):
                                mm.then_inc(z_done, 1)

                    pe.wait_ge(qklo_made, hh * UNITS + 10)
                    scores(0, (0,))
                    pe.wait_ge(qklo_made, (hh + 1) * UNITS)
                    scores(0, (1,))
                    scores(1)
                    turn_p(0)
                    def start_with_h(c):
                        nc.tensor.matmul(ps[:, wo_bank[c], :], ident[:, :], h[:, bass.ds(hf * 2 + c, 1), :].rearrange("p a n -> p (a n)"),
                                         start=True, stop=False, skip_group_check=True)

                    for b in range(HB):
                        if b + 2 < HB:
                            scores(b + 2)
                        if b == HB - 2:
                            start_with_h(0)
                            pe.wait_ge(plo_made, nb + (HB - 1))
                            turn_p(HB - 1)
                        mix(b)
                        if b + 1 < HB - 1:
                            turn_p(b + 1)
                    pe.wait_ge(zlo_made, z_count(hh, HB - 2))
                    start_with_h(1)
                    pe.wait_ge(wlo_made, (tile_of(l, 2) + 1) * 2)
                    pe.wait_ge(zlo_made, z_count(hh, HB - 1, False))
                    firsts, others = (0, 1), (2, 3)
                    order = [(0, 0, firsts), (1, 0, firsts), (0, 0, others), (0, 1, firsts + others), (1, 0, others), (1, 1, firsts + others)]
                    order += [(j, e, firsts + others) for j in (2, 3) for e in range(2)]
                    for n, (j, e, chunks) in enumerate(order):
                        if n == 2:
                            pe.wait_ge(zlo_made, z_count(hh, HB - 1))
                        for dc in chunks:
                            cols = slice(j * P, (j + 1) * P)
                            mm = three(ps[:, o_bank[j], e * HN:(e + 1) * HN],
                                       split3(slot(SA, 0)[:, dc, cols], slot(SA, 1)[:, dc, cols],
                                              qz[0][:, dc, :, 2 * j + e, :], qz[1][:, dc, :, 2 * j + e, :]),
                                       dc == 0, dc == DC - 1)
                        if e == 1:
                            mm.then_inc(o_done, 1)
                    pe.wait_ge(wlo_made, (tile_of(l, 3) + 1) * 2)
                    for c in range(2):
                        cols = slice(c * P, (c + 1) * P)
                        for j in range(HP):
                            pe.wait_ge(olo_made, hh * HP + (j + 1))
                            mm = add3(ps[:, wo_bank[c], :], split3(o_hi[:, j, cols], o_lo[:, j, cols], slot(SB_, 0)[:, j, :], slot(SB_, 1)[:, j, :]),
                                      j == HP - 1)
                        mm.then_inc(wo_done, 1)
                def ff_from_h(c):
                    nc.tensor.matmul(ps[:, 4 + c, :], ident[:, :], h[:, c, :], start=True, stop=False, skip_group_check=True)

                ff_from_h(1)
                pe.wait_ge(h_new, l * 8 + 7)
                for c in range(NC):
                    pe.wait_ge(xn_made, l * 8 + (c + 9))
                    turn_chunk(xn, c)
                    if c == 2:
                        ff_from_h(c)
                pe.wait_ge(h_new, l * 8 + 8)
                ff_from_h(0)
                ff_from_h(3)
                with pe.Fori(0, FI) as i:
                    n0 = l * (FI * FJ) + i * FJ
                    for j in range(FJ):
                        s = SB_ if j < 2 else SC
                        g_tile = tile_of(l, 4) + i * 3 + j // 2
                        if j == 0:
                            pe.wait_ge(wlo_made, g_tile * 2 + 1)
                        if j == 2:
                            pe.wait_ge(wlo_made, g_tile * 2 + 2)
                        if j >= 2:
                            pe.wait_ge(prod_made, n0 + (j - 1))

                        def columns(vg):
                            return slice(vg * 256 + (j % 2) * P, vg * 256 + (j % 2 + 1) * P)

                        if j == 0:
                            pe.wait_ge(yf_made, y_first(l, 2) + 2)
                            for k in range(DC):
                                pe.wait_ge(yhi_made, y_first(l, 2) + (k + 1))
                                if k == 2:
                                    pe.wait_ge(wlo_made, g_tile * 2 + 2)
                                for vg in (1, 0):
                                    for w in range(2):
                                        nc.tensor.matmul(ps[:, vg, :], slot(s, w)[:, k, columns(vg)], y_hi[:, k, :],
                                                         start=k == 0 and w == 0, stop=False)
                                pe.wait_ge(ylo_made, y_first(l, 2) + (k + 1))
                                for vg in (1, 0):
                                    mm = nc.tensor.matmul(ps[:, vg, :], slot(s, 0)[:, k, columns(vg)], y_lo[:, k, :],
                                                          start=False, stop=k == DC - 1)
                                    if k == DC - 1:
                                        mm.then_inc(gate_done if vg else val_done, 1)
                        else:
                            for vg in (1, 0):
                                for k in range(DC):
                                    mm = three(ps[:, 2 * (j % 2) + vg, :],
                                               split3(slot(s, 0)[:, k, columns(vg)], slot(s, 1)[:, k, columns(vg)], y_hi[:, k, :], y_lo[:, k, :]),
                                               k == 0, k == DC - 1)
                                mm.then_inc(gate_done if vg else val_done, 1)
                    pe.wait_ge(wlo_made, (tile_of(l, 6) + i * 3 + 1) * 2)
                    for j, c in ([(j, c) for j in range(FJ) for c in (0, 1)] + [(j, c) for c in (2, 3) for j in range(FJ)]):
                        pe.wait_ge(flo_made, n0 + (j + 1))
                        cols = slice(c * P, (c + 1) * P)
                        mm = add3(ps[:, 4 + c, :], split3(fT_hi[:, j, cols], fT_lo[:, j, cols], slot(SA, 0)[:, j, :], slot(SA, 1)[:, j, :]),
                                  j == FJ - 1)
                        if j == FJ - 1:
                            mm.then_inc(ff_done, 1)

                start_layer(l + 1)

            pe.wait_ge(yf_made, y_first(L, 1))
            turn(h, h_new, lambda c: 8 * L + 4 - NC + c + 1)
            project(SB_, NT - 1, 4, y_first(L, 1))
            pe.wait_ge(back_in, 48)
            spread(0, NC)


def kernel(**inputs):
    import numpy as np
    import concourse.bacc as bacc
    from concourse.bass_utils import run_bass_kernel_spmd as run

    g = {k.replace("L0_gnn_", ""): np.asarray(v) for k, v in inputs.items()}

    def rows_tile(w):
        return w.reshape(4, P, 512).transpose(1, 0, 2).reshape(P, TILE)

    tiles = [rows_tile(g["gcn_in_w"])]
    for l in range(L):
        tiles += [rows_tile(g["Wq"][l]), rows_tile(g["Wk"][l].T), rows_tile(g["Wv"][l]), rows_tile(g["Wo"][l])]
        gg = g["geglu_w"][l].reshape(DC, P, 2, 2 * FI, 256).transpose(3, 1, 0, 2, 4).reshape(2 * FI, P, TILE)
        ff = g["ffo_w"][l].reshape(FI, FJ, P, D).transpose(0, 2, 1, 3).reshape(FI, P, TILE)
        for i in range(FI):
            tiles += [gg[2 * i], gg[2 * i + 1], ff[i]]
    tiles.append(rows_tile(g["gcn_out_w"]))
    tiles.append(tiles[-1])
    cond = g["cond"]
    arrays = {
        "x": g["x"], "src": g["src"], "dst": g["dst"],
        "tiles": np.stack(tiles),
        "cond_n": cond.reshape(HALVES, HB, 2, P, D).transpose(0, 1, 3, 2, 4).reshape(HALVES, HB, P, 2 * D),
        "cond_t": cond.transpose(0, 2, 1).reshape(HALVES, HB, DC, P, M).transpose(0, 1, 3, 2, 4).reshape(HALVES, HB, P, DC * M),
        "bn_p": np.stack([g["bn_w"].reshape(DC, P).T, g["bn_b"].reshape(DC, P).T], axis=-1),
        "ln_p": np.stack([np.stack([g["ln2_w"], g["ln3_w"]], 1), np.stack([g["ln2_b"], g["ln3_b"]], 1)], -1)
                .reshape(L, 2, DC, P, 2).transpose(3, 0, 1, 2, 4).reshape(P, L * 2 * DC * 2),
        "gb_p": g["geglu_b"].reshape(L, 2, FI, FJ, P).transpose(4, 0, 2, 3, 1).reshape(P, L * FI * FJ * 2),
        "rows": np.concatenate([g["gcn_in_b"][None], g["ffo_b"], g["gcn_out_b"][None]]),
    }
    arrays["ln_p"] = np.concatenate([arrays["ln_p"], arrays["ln_p"][:, -2 * DC * 2:]], axis=1)
    arrays = {k: np.ascontiguousarray(v) for k, v in arrays.items()}
    nc = bacc.Bacc("TRN2", target_bir_lowering=False, num_devices=1)
    args = [nc.dram_tensor(k, v.shape, mybir.dt.from_np(v.dtype), kind="ExternalInput").ap() for k, v in arrays.items()]
    out = nc.dram_tensor("out", (N, D), mybir.dt.float32, kind="ExternalOutput").ap()
    adj_hi = nc.dram_tensor("adj_hi", (P, NC, N), mybir.dt.float32, kind="Internal").ap()
    adj_lo = nc.dram_tensor("adj_lo", (P, NC, N), mybir.dt.float32, kind="Internal").ap()
    rest = nc.dram_tensor("rest", (P, NC, D), mybir.dt.float32, kind="Internal").ap()
    build(nc, *args, out, adj_hi, adj_lo, rest)
    return run(nc, [arrays], core_ids=[0]).results[0]["out"]
```
